# Optimizing a Trainium2 kernel written in Bass

```python
import numpy as np
import jax
import jax.numpy as jnp

def _softmax(x, axis=-1):
    return jax.nn.softmax(x, axis=axis)

def _gelu(x):
    return jax.nn.gelu(x, approximate=True)

def _silu(x):
    return jax.nn.silu(x)

def _sigmoid(x):
    return jax.nn.sigmoid(x)

def _layernorm(x, axis=-1, eps=1e-05):
    m = jnp.mean(x, axis=axis, keepdims=True)
    v = jnp.var(x, axis=axis, keepdims=True)
    return (x - m) / jnp.sqrt(v + eps)

def _scatter_add(tgt, idx, src, axis=0):
    return tgt.at[idx].add(src)

def _segment_sum(src, seg, n):
    return jax.ops.segment_sum(src, seg, n)
kernel_name = 'mk_macaron_d1_jaxref_r8_df00b2'

def setup_inputs(seed: int=0):
    np.random.seed(seed)
    _w = jnp.asarray

    def _L0_attn_setup():
        import jax, jax.numpy as jnp
        import numpy as np
        D_MODEL = 128
        key = jax.random.key(seed)
        k1, k2, k3, k4 = jax.random.split(key, 4)
        B, T, D, E = (8, 256, 128, 128)
        x = jax.random.normal(k1, (B, T, D), dtype=jnp.float32)
        Wq = jax.random.normal(k2, (D, E), dtype=jnp.float32) * (1.0 / np.sqrt(D))
        Wk = jax.random.normal(k3, (D, E), dtype=jnp.float32) * (1.0 / np.sqrt(D))
        Wv = jax.random.normal(k4, (D, E), dtype=jnp.float32) * (1.0 / np.sqrt(D))
        return {'x': x, 'Wq': Wq, 'Wk': Wk, 'Wv': Wv}
    _L0_attn_in = _L0_attn_setup()

    def _L0_ffn_setup():
        import jax, jax.numpy as jnp
        import numpy as np
        B, S, H, NH, E, F = (4, 128, 128, 16, 8, 512)
        D = H // NH
        EPS = 1e-05

        def _layernorm(x, g, b):
            mu = jnp.mean(x, axis=-1, keepdims=True)
            var = jnp.var(x, axis=-1, keepdims=True)
            return (x - mu) * jax.lax.rsqrt(var + EPS) * g + b
        key = jax.random.key(seed)
        ks = jax.random.split(key, 16)
        s = 0.02
        return {'x': jax.random.normal(ks[0], (B, S, H), jnp.float32), 'ln1_g': jnp.ones((H,), jnp.float32), 'ln1_b': jnp.zeros((H,), jnp.float32), 'ln2_g': jnp.ones((H,), jnp.float32), 'ln2_b': jnp.zeros((H,), jnp.float32), 'wq': jax.random.normal(ks[1], (H, H), jnp.float32) * s, 'bq': jnp.zeros((H,), jnp.float32), 'wk': jax.random.normal(ks[2], (H, H), jnp.float32) * s, 'bk': jnp.zeros((H,), jnp.float32), 'wv': jax.random.normal(ks[3], (H, H), jnp.float32) * s, 'bv': jnp.zeros((H,), jnp.float32), 'wo': jax.random.normal(ks[4], (H, H), jnp.float32) * s, 'bo': jnp.zeros((H,), jnp.float32), 'gate_w': jax.random.normal(ks[5], (H, E), jnp.float32) * s, 'gate_b': jnp.zeros((E,), jnp.float32), 'w1': jax.random.normal(ks[6], (E, H, F), jnp.float32) * s, 'b1': jnp.zeros((E, F), jnp.float32), 'w2': jax.random.normal(ks[7], (E, F, H), jnp.float32) * s, 'b2': jnp.zeros((E, H), jnp.float32)}
    _L0_ffn_in = _L0_ffn_setup()
    _d = {'L0_attn_x': _L0_attn_in['x'], 'L0_attn_Wq': _L0_attn_in['Wq'], 'L0_attn_Wk': _L0_attn_in['Wk'], 'L0_attn_Wv': _L0_attn_in['Wv'], 'L0_ffn_ln1_g': _L0_ffn_in['ln1_g'], 'L0_ffn_ln1_b': _L0_ffn_in['ln1_b'], 'L0_ffn_ln2_g': _L0_ffn_in['ln2_g'], 'L0_ffn_ln2_b': _L0_ffn_in['ln2_b'], 'L0_ffn_wq': _L0_ffn_in['wq'], 'L0_ffn_bq': _L0_ffn_in['bq'], 'L0_ffn_wk': _L0_ffn_in['wk'], 'L0_ffn_bk': _L0_ffn_in['bk'], 'L0_ffn_wv': _L0_ffn_in['wv'], 'L0_ffn_bv': _L0_ffn_in['bv'], 'L0_ffn_wo': _L0_ffn_in['wo'], 'L0_ffn_bo': _L0_ffn_in['bo'], 'L0_ffn_gate_w': _L0_ffn_in['gate_w'], 'L0_ffn_gate_b': _L0_ffn_in['gate_b'], 'L0_ffn_w1': _L0_ffn_in['w1'], 'L0_ffn_b1': _L0_ffn_in['b1'], 'L0_ffn_w2': _L0_ffn_in['w2'], 'L0_ffn_b2': _L0_ffn_in['b2']}
    _x0 = _d['L0_attn_x']
    _d['L0_attn_x'] = jax.random.normal(jax.random.fold_in(jax.random.key(seed), 1), (4, 512, 128), dtype=_x0.dtype)
    del _x0
    return _d

def reference(L0_attn_x, L0_attn_Wq, L0_attn_Wk, L0_attn_Wv, L0_ffn_ln1_g, L0_ffn_ln1_b, L0_ffn_ln2_g, L0_ffn_ln2_b, L0_ffn_wq, L0_ffn_bq, L0_ffn_wk, L0_ffn_bk, L0_ffn_wv, L0_ffn_bv, L0_ffn_wo, L0_ffn_bo, L0_ffn_gate_w, L0_ffn_gate_b, L0_ffn_w1, L0_ffn_b1, L0_ffn_w2, L0_ffn_b2):

    def _L0_attn_ref(x, Wq, Wk, Wv):
        import jax, jax.numpy as jnp
        import numpy as np
        D_MODEL = 128
        T = x.shape[1]
        Q = x @ Wq
        K = x @ Wk
        V = x @ Wv
        scale = 1.0 / jnp.sqrt(jnp.asarray(D_MODEL, dtype=x.dtype))
        w = jnp.einsum('bte,bse->bts', Q, K) * scale
        causal = jnp.tril(jnp.ones((T, T), dtype=bool))
        w = jnp.where(causal, w, -jnp.inf)
        w = jax.nn.softmax(w, axis=-1)
        return w @ V

    def _L0_ffn_ref(x, ln1_g, ln1_b, ln2_g, ln2_b, wq, bq, wk, bk, wv, bv, wo, bo, gate_w, gate_b, w1, b1, w2, b2):
        import jax, jax.numpy as jnp
        import numpy as np
        B, S, H, NH, E, F = (4, 128, 128, 16, 8, 512)
        D = H // NH
        EPS = 1e-05

        def _layernorm(x, g, b):
            mu = jnp.mean(x, axis=-1, keepdims=True)
            var = jnp.var(x, axis=-1, keepdims=True)
            return (x - mu) * jax.lax.rsqrt(var + EPS) * g + b
        b, s, h = x.shape
        hn = _layernorm(x, ln1_g, ln1_b)
        q = (hn @ wq + bq).reshape(b, s, NH, D).transpose(0, 2, 1, 3)
        k = (hn @ wk + bk).reshape(b, s, NH, D).transpose(0, 2, 1, 3)
        v = (hn @ wv + bv).reshape(b, s, NH, D).transpose(0, 2, 1, 3)
        scores = jnp.einsum('bhqd,bhkd->bhqk', q, k) / jnp.sqrt(jnp.float32(D))
        attn = jax.nn.softmax(scores, axis=-1)
        o = jnp.einsum('bhqk,bhkd->bhqd', attn, v)
        o = o.transpose(0, 2, 1, 3).reshape(b, s, h)
        x = x + (o @ wo + bo)
        hn2 = _layernorm(x, ln2_g, ln2_b).reshape(-1, h)
        logits = hn2 @ gate_w + gate_b
        idx = jnp.argmax(logits, axis=-1)
        mid = jax.nn.relu(jnp.einsum('th,ehf->etf', hn2, w1) + b1[:, None, :])
        y = jnp.einsum('etf,efh->eth', mid, w2) + b2[:, None, :]
        moe = y[idx, jnp.arange(hn2.shape[0])]
        return x + moe.reshape(b, s, h)
    x = L0_attn_x
    x = x + 0.5 * _L0_ffn_ref(_layernorm(x, axis=-1), L0_ffn_ln1_g, L0_ffn_ln1_b, L0_ffn_ln2_g, L0_ffn_ln2_b, L0_ffn_wq, L0_ffn_bq, L0_ffn_wk, L0_ffn_bk, L0_ffn_wv, L0_ffn_bv, L0_ffn_wo, L0_ffn_bo, L0_ffn_gate_w, L0_ffn_gate_b, L0_ffn_w1, L0_ffn_b1, L0_ffn_w2, L0_ffn_b2)
    x = x + _L0_attn_ref(_layernorm(x, axis=-1), L0_attn_Wq, L0_attn_Wk, L0_attn_Wv)
    x = x + 0.5 * _L0_ffn_ref(_layernorm(x, axis=-1), L0_ffn_ln1_g, L0_ffn_ln1_b, L0_ffn_ln2_g, L0_ffn_ln2_b, L0_ffn_wq, L0_ffn_bq, L0_ffn_wk, L0_ffn_bk, L0_ffn_wv, L0_ffn_bv, L0_ffn_wo, L0_ffn_bo, L0_ffn_gate_w, L0_ffn_gate_b, L0_ffn_w1, L0_ffn_b1, L0_ffn_w2, L0_ffn_b2)
    return x

_drawn_inputs = setup_inputs


def setup_inputs(seed=0):
    import zlib

    import numpy as np

    out = dict(_drawn_inputs(seed))
    spreads = {'L0_ffn_ln1_g': (1.0, 0.6),
     'L0_ffn_ln1_b': (0.0, 0.8),
     'L0_ffn_ln2_g': (1.0, 0.2),
     'L0_ffn_ln2_b': (0.0, 0.403),
     'L0_ffn_bq': (0.0, 0.8),
     'L0_ffn_bk': (0.0, 0.8),
     'L0_ffn_bv': (0.0, 0.442),
     'L0_ffn_bo': (0.0, 0.1),
     'L0_ffn_gate_b': (0.0, 0.1),
     'L0_ffn_b1': (0.0, 0.45),
     'L0_ffn_b2': (0.0, 0.1)}
    factors = {'L0_ffn_wq': 8.0, 'L0_ffn_wk': 8.0, 'L0_ffn_wv': 7.476, 'L0_ffn_wo': 3.194}
    for name, (base, spread) in spreads.items():
        noise = np.random.default_rng([zlib.crc32(name.encode()), seed]).standard_normal(out[name].shape)
        drawn = base * np.exp(spread * noise) if base else spread * noise
        out[name] = jnp.asarray(drawn.astype(out[name].dtype))
    for name, factor in factors.items():
        out[name] = (out[name] * factor).astype(out[name].dtype)
    return out
```

```python
from contextlib import ExitStack

import numpy as np

import concourse.bass as bass
from concourse import mybir

F32 = mybir.dt.float32
BF16 = mybir.dt.bfloat16
I32 = mybir.dt.int32
U32 = mybir.dt.uint32
ALU = mybir.AluOpType
ACT = mybir.ActivationFunctionType
AX = mybir.AxisListType

P = 128
B, T = 4, 512
TT = T // P
NT = B * TT
NH, HD = 16, 8
E, F = 8, 512
FC = F // P
EPS = 1e-5
GROUP = 4
GROUPS = NH // GROUP
PARTS = 3
Q_PART = (0, 0, 1, 1, 0, 2)
K_PART = (0, 1, 0, 1, 2, 0)
STACK = len(Q_PART) * HD
SROWS = 2 * STACK
VW = HD + 1
TILES = NT + E - 1
TILES += TILES % 2
LDQK = 2 * 2 * len(Q_PART)

_AT, _W = {}, 0
for _name, _n in (("ident", P), ("wq", P), ("wk", P), ("wv", P), ("wo", P), ("aq", P), ("ak", P), ("av", P),
                  ("bv", P), ("bo", P), ("causal", P), ("before", P), ("ones", P), ("gate_w", E), ("gate_b", E),
                  ("g1", 1), ("b1", 1), ("g2", 1), ("b2", 1), ("bq", 1), ("bk", 1), ("iota", E), ("tile", 24)):
    _AT[_name] = (_W, _W + _n)
    _W += _n
PARAMS = _W
EW = F + FC * P + FC + P


class Tally:

    def __init__(self, sem):
        self.sem, self.n, self.base, self.per = sem, 0, None, 0

    def add(self, ins, by=1):
        ins.then_inc(self.sem, by)
        self.n += by
        return ins

    def now(self):
        return self.n if self.base is None else self.base + self.n

    def enter(self, i, per):
        self.base, self.per, self.start = i * per, per, self.n

    def leave(self, rounds):
        assert self.n - self.start == self.per, (self.n - self.start, self.per)
        self.n = self.start + rounds * self.per
        self.base = None


def ring_entries():
    order = {}

    def put(*key):
        order[key] = len(order)

    for k in range(2 * GROUPS):
        for u in range(8):
            if k < 2 * GROUPS - 1 or u < 4:
                for y in range(2):
                    put("max", *lookahead(k, u, y))
            if u == 3 and k:
                put("oT", k - 1)
            if u == 5:
                put("mT", k + 1)
            if u == 6 and k == GROUPS:
                put("OT", 0)
            if u == 7 and k == GROUPS:
                put("wo", 0)
    k = 2 * GROUPS - 1
    for y in range(8):
        put("max", k + 2, y // TT, y % TT)
    put("oT", k)
    put("OT", 1)
    put("wo", 1)
    return order


def lookahead(k, u, y):
    e = 2 * u + y
    if u < 4:
        return k + 1, (8 + e) // TT, (8 + e) % TT
    return k + 2, (e - 8) // TT, (e - 8) % TT


RING = ring_entries()
PER = len(RING)
PRO = 16 + 1 + 8
ORDER = list(RING)
DVE_READ = {key: sum(o[0] != "mT" for o in ORDER[:r + 1]) for key, r in RING.items()}
DPER = PER - 2 * GROUPS
DPRO = PRO - 1
assert PER % 2 == 0


def program(nc, x, params, experts, out):
    with ExitStack() as ctx:
        def sb(name, shape, dt=F32):
            return ctx.enter_context(nc.sbuf_tensor(name, shape, dt))

        def sem(name):
            return ctx.enter_context(nc.semaphore(name))

        q_dram = nc.dram_tensor("q_parts", (B, P, PARTS, T), BF16).ap()
        k_dram = nc.dram_tensor("k_parts", (B, P, PARTS, T), BF16).ap()
        xs_dram = nc.dram_tensor("sorted_in", (TILES * P, P), F32).ap()
        ys_dram = nc.dram_tensor("sorted_out", (TILES * P, P), F32).ap()

        par = sb("par", [P, PARAMS])
        X = sb("X", [P, NT, P])
        U = sb("U", [P, NT, P])
        N = sb("N", [P, NT, P])
        Nb = sb("Nb", [P, TT, P])
        Y = sb("Y", [P, NT, P])
        stats = sb("stats", [P, NT, 6])
        mv = sb("mv", [P, NT, 2])
        rstd = sb("rstd", [P, NT, 1])
        nhalf = sb("nhalf", [P, NT])
        hT = sb("hT", [P, T])
        full = sb("full", [P, 2, T])
        rest = sb("rest", [P, 2, T])
        parts = sb("parts", [P, 2, PARTS, T], BF16)
        Vall = sb("Vall", [P, B, TT * NH * VW])
        Qs = [sb(f"Qs{i}", [P, NH, T], BF16) for i in range(2)]
        Ks = [sb(f"Ks{i}", [P, NH // 2, T], BF16) for i in range(2)]
        Vs = [sb(f"Vs{i}", [P, TT, NH, VW]) for i in range(2)]
        M = sb("M", [P, 2, TT, GROUP])
        Mr = sb("Mr", [P, TT, GROUP])
        Mp = sb("Mp", [P, 2, TT, PARTS, GROUP], BF16)
        MT = sb("MT", [PARTS * GROUP, 2, T], BF16)
        Pb = sb("Pb", [P, 8, 2, T])
        oS = sb("oS", [P, 2, T])
        rden = sb("rden", [P, TT, GROUP, 1])
        O = sb("O", [P, TT, P])
        OT = sb("OT", [P, T])
        tmp = sb("tmp", [P, TT, P])
        W = [sb(f"W{i}", [P, EW]) for i in range(2)]
        xt = [sb(f"xt{i}", [P, P]) for i in range(2)]
        xT = [sb(f"xT{i}", [P, P]) for i in range(2)]
        mid = [sb(f"mid{i}", [P, FC, P]) for i in range(2)]
        yt = [sb(f"yt{i}", [P, P]) for i in range(2)]
        identb = sb("identb", [P, P], BF16)
        L = sb("L", [P, NT, E])
        L2 = sb("L2", [P, NT, E])
        mx = sb("mx", [P, NT, 1])
        hot = sb("hot", [P, NT, E])
        cumA = sb("cumA", [P, NT, E])
        cumB = sb("cumB", [P, NT, E])
        nt = sb("nt", [P, E])
        nti = sb("nti", [P, E], I32)
        ends = sb("ends", [P, 2, E])
        slotf = sb("slotf", [P, NT])
        slot = sb("slot", [P, NT], U32)
        owner = sb("owner", [P, 24, E])
        ownf = sb("ownf", [P, 24])
        owni = sb("owni", [P, 24], I32)
        AT_p = Pb[:, 0:2, :, :].rearrange("p a b t -> p (a b) t")
        AT_pT = Pb[:, 2:4, :, :].rearrange("p a b t -> p (a b) t")
        AT_q, AT_k = Pb[:, 4, 0, :], Pb[:, 4, 1, :]
        AT_v = Pb[:, 5, 0, :].rearrange("p (c d) -> p c d", d=P)
        hT2 = Pb[:, 6:8, :, :].rearrange("p a b t -> p (a b) t")
        amx = sb("amx", [P, TT])
        asum = sb("asum", [P, TT])
        arec = sb("arec", [P, TT])
        PS = ctx.enter_context(nc.psum_tensor("PS", [P, 8, T], F32))

        def pr(name, rows=P):
            a, b = _AT[name]
            return par[0:rows, a:b]

        S = {n: sem(n) for n in (
            "loaded", "x_stored", "zeroed", "setup_done", "dve_step", "pool_step",
            "stat_done", "rstd_ready", "rows_ready",
            "hT_filled", "hT_ready", "qkv_filled", "v_read", "qk_read", "mids_ready", "rests_ready", "parts_ready",
            "parts_stored", "qk_loaded0", "qk_loaded1", "v_loaded0", "v_loaded1",
            "ring_full", "ring_read", "maxT_ready", "max_split", "max_loaded",
            "scores_full", "exp_done", "pv_done", "o_read",
            "hT2_ready", "logits_full", "hot_ready", "ranks_full", "slots_ready", "scattered",
            "w_loaded0", "w_loaded1", "xt_full", "xT_ready", "mid_full", "mid_ready", "y_full", "y_ready",
            "y_stored0", "y_stored1", "gathered", "ffn_done",
            "a_qkv_full", "a_qk_read", "a_v_read", "a_s_full", "a_max", "a_exp", "a_pT_full", "a_pT_read",
            "a_o_full", "attn_done")}

        def link(eng, tally, ins):
            tally.add(ins)
            eng.wait_ge(tally.sem, tally.now())

        block = ctx.enter_context(nc.Block())

        @block.sync
        def _(sp):
            sp.dma_start(par[:, :], params).then_inc(S["loaded"], 16)
            sp.dma_start(X[:, :, :], x.rearrange("(t p) d -> p t d", p=P)).then_inc(S["loaded"], 16)
            sp.wait_ge(S["setup_done"], 1)
            sp.dma_start(xs_dram.rearrange("(j p) d -> p j d", p=P)[:, 0:12, :], U[:, 0:12, :]).then_inc(S["zeroed"], 16)
            sp.dma_start(xs_dram.rearrange("(j p) d -> p j d", p=P)[:, 12:24, :], U[:, 0:12, :]).then_inc(S["zeroed"], 16)

            def load_stacks(i, b):
                for src, dst, pick in ((q_dram, Qs[i], Q_PART), (k_dram, Ks[i], K_PART)):
                    for r in range(2):
                        for g, part in enumerate(pick):
                            rows = slice(r * STACK + g * HD, r * STACK + (g + 1) * HD)
                            v = src[bass.ds(b, 1), :, part, :].rearrange("o (s r d) t -> d s (o r) t", r=2, d=HD)[:, :, r, :]
                            to = dst[rows, r::2, :] if dst is Qs[i] else dst[rows, :, :]
                            sp.dma_start(to, v).then_inc(S[f"qk_loaded{i}"], 16)
                sp.dma_start(Vs[i][:, :, :, :].rearrange("p c h w -> p (c h w)"),
                             Vall[:, bass.ds(b, 1), :].rearrange("p o w -> p (o w)")).then_inc(S[f"v_loaded{i}"], 16)

            def load_max(n, buf, i, h0):
                sp.wait_ge(S["maxT_ready"], n)
                for p in range(PARTS):
                    sp.dma_start(Qs[i][SROWS + p:SROWS + p + 1, h0:h0 + GROUP, :],
                                 MT[p * GROUP:(p + 1) * GROUP, buf, :]).then_inc(S["max_loaded"], 16)

            def load_tile(j, i):
                e = sp.value_load(owni[0:1, bass.ds(j, 1)], min_val=0, max_val=E - 1)
                sp.dma_start(W[i][:, :], experts[bass.ds(e, 1), :, :].rearrange("o p w -> p (o w)")).then_inc(S[f"w_loaded{i}"], 16)
                sp.dma_start(xt[i][:, :], xs_dram[bass.ds(j * P, P), :]).then_inc(S[f"w_loaded{i}"], 16)

            def store_tile(j, i, ready):
                sp.wait_ge(S["y_ready"], ready)
                sp.dma_start(ys_dram[bass.ds(j * P, P), :], yt[i][:, :]).then_inc(S[f"y_stored{i}"], 16)

            for layer in range(2):
                with sp.Fori(0, B) as b:
                    sp.wait_ge(S["parts_ready"], b * 2 + (2 + layer * 2 * B))
                    for j, dst in ((0, q_dram), (1, k_dram)):
                        sp.dma_start(dst[bass.ds(b, 1), :, :, :].rearrange("o p a t -> p (o a) t"),
                                     parts[:, j, :, :]).then_inc(S["parts_stored"], 16)
                sp.wait_ge(S["parts_stored"], 32 * (B * (layer + 1) + 1))
                sp.wait_ge(S["v_read"], B * (layer + 1) + 1)
                if layer:
                    sp.wait_ge(S["ring_full"], layer * (PRO + 2 * PER))
                load_stacks(0, 0)
                mt = layer * (1 + 2 * 2 * GROUPS)
                load_max(mt + 1, 0, 0, 0)
                with sp.Fori(0, 2) as it:
                    for k in range(2 * GROUPS):
                        if k == 0:
                            sp.wait_ge(S["pv_done"], it * (4 * GROUPS) + (2 + layer * 8 * GROUPS))
                            load_stacks(1, it * 2 + 1)
                        if k == GROUPS:
                            sp.wait_ge(S["pv_done"], it * (4 * GROUPS) + (2 + 2 * GROUPS + layer * 8 * GROUPS))
                            load_stacks(0, it * (-2) + 2)
                        kk = k + 1
                        load_max(it * (2 * GROUPS) + (mt + 1 + kk), kk % 2, (kk // GROUPS) % 2, (kk % GROUPS) * GROUP)
                sp.wait_ge(S["max_loaded"], 16 * PARTS * (1 + 4 * GROUPS) * (layer + 1))
                sp.wait_ge(S["slots_ready"], layer + 1)
                sp.wait_ge(S["scattered"], 16 * NT * (layer + 1))
                for i in range(2):
                    load_tile(i, i)
                with sp.Fori(0, TILES // 2 - 1) as it:
                    for i in range(2):
                        store_tile(it * 2 + i, i, it * 2 + (1 + i + layer * TILES))
                        load_tile(it * 2 + (2 + i), i)
                for i in range(2):
                    store_tile(TILES - 2 + i, i, (layer + 1) * TILES - 1 + i)

            sp.wait_ge(S["ffn_done"], 2 * 4)
            sp.dma_start(out.rearrange("(t p) d -> p t d", p=P), X[:, :, :]).then_inc(S["x_stored"], 16)
            sp.wait_ge(S["x_stored"], 16)

        @block.gpsimd
        def _(pool):
            step = Tally(S["pool_step"])
            link(pool, step, nc.gpsimd.memset(nhalf[:, :], -0.5))

            def inverse_deviations(n):
                pool.wait_ge(S["stat_done"], NT * n)
                link(pool, step, nc.gpsimd.tensor_scalar(rstd[:, :, 0], mv[:, :, 1], EPS, 1.0, ALU.add, ALU.mult))
                nc.gpsimd.tensor_tensor(rstd[:, :, 0], rstd[:, :, 0], nhalf[:, :], ALU.pow).then_inc(S["rstd_ready"], 1)

            n = 0
            for layer in range(2):
                for _ in range(3):
                    n += 1
                    inverse_deviations(n)
                pool.wait_ge(S["zeroed"], 32)
                pool.wait_ge(S["slots_ready"], layer + 1)
                for t in range(NT):
                    nc.gpsimd.indirect_dma_start(xs_dram, bass.IndirectOffsetOnAxis(slot[:, t:t + 1], 0),
                                                 N[:, t, :], None).then_inc(S["scattered"], 16)
                for i in range(2):
                    pool.wait_ge(S[f"y_stored{i}"], 16 * (TILES // 2 * (layer + 1) + 1))
                for t in range(NT):
                    nc.gpsimd.indirect_dma_start(Y[:, t, :], None, ys_dram,
                                                 bass.IndirectOffsetOnAxis(slot[:, t:t + 1], 0)).then_inc(S["gathered"], 16)
                if layer == 0:
                    n += 1
                    inverse_deviations(n)

        @block.tensor
        def _(pe):
            ident = pr("ident")
            mm = nc.tensor.matmul
            pe.wait_ge(S["loaded"], 32)
            pe.wait_ge(S["setup_done"], 1)

            def stage_prep(layer):
                with pe.Fori(0, B) as b:
                    n = b + (1 + layer * B)
                    turned = b + (1 + layer * 2 * B)
                    pe.wait_ge(S["hT_ready"], turned)
                    pe.wait_ge(S["rows_ready"], b + (layer * (2 * B + 1) + 1))
                    for c in range(TT):
                        last = nc.tensor.transpose(PS[:, 0, c * P:(c + 1) * P], Nb[:, c, :], ident)
                    last.then_inc(S["hT_filled"], 1)
                    pe.wait_ge(S["hT_ready"], turned + 1)
                    pe.wait_ge(S["qk_read"], n * 4)
                    mm(PS[:, 1, :], pr("wq"), hT[:, :], start=True, stop=True).then_inc(S["qkv_filled"], 1)
                    mm(PS[:, 2, :], pr("wk"), hT[:, :], start=True, stop=True).then_inc(S["qkv_filled"], 1)
                    pe.wait_ge(S["v_read"], n)
                    for c in range(TT):
                        last = mm(PS[:, 3, c * P:(c + 1) * P], hT[:, c * P:(c + 1) * P], pr("wv"), start=True, stop=True)
                    last.then_inc(S["qkv_filled"], 1)

            def max_scores(slot_, i, h, c):
                return mm(PS[:, slot_, :], Qs[i][0:SROWS, h, c * P:(c + 1) * P], Ks[i][0:SROWS, h // 2, :],
                          start=True, stop=True)

            def max_columns(slot_, buf):
                bank = PS[0:PARTS * GROUP, slot_, :].bitcast(BF16)
                for c in range(TT):
                    last = nc.tensor.transpose(bank[:, c * P:(c + 1) * P],
                                               Mp[:, buf, c, :, :].rearrange("p a j -> p (a j)"), identb[:, :])
                return last

            def stage_heads(layer):
                start = layer * (PRO + 2 * PER)
                splits = layer * (1 + 2 * 2 * GROUPS)
                r0 = PRO % 2

                read0 = layer * (DPRO + 2 * DPER)

                pe.wait_ge(S["qk_loaded0"], layer * 3 * 16 * LDQK + 16 * LDQK)
                for e in range(16):
                    if e >= 2:
                        pe.wait_ge(S["ring_read"], read0 + e - 1)
                    max_scores(e % 2, 0, e // TT, e % TT).then_inc(S["ring_full"], 1)
                pe.wait_ge(S["ring_read"], read0 + 15)
                pe.wait_ge(S["max_split"], splits + 1)
                max_columns(0, 0).then_inc(S["ring_full"], 1)
                for e in range(8):
                    if e == 1:
                        pe.wait_ge(S["maxT_ready"], splits + 1)
                    else:
                        pe.wait_ge(S["ring_read"], read0 + 16 + max(e - 1, 0))
                    max_scores((17 + e) % 2, 0, GROUP + e // TT, e % TT).then_inc(S["ring_full"], 1)

                with pe.Fori(0, 2) as it:
                    def fill(key):
                        r = RING[key]
                        before = ORDER[r - 2]
                        if r >= 2 and before[0] == "mT":
                            pe.wait_ge(S["maxT_ready"], it * (2 * GROUPS) + (splits + 1 + before[1]))
                        else:
                            n = DVE_READ[before] if r >= 2 else r - 1
                            pe.wait_ge(S["ring_read"], it * DPER + (read0 + DPRO + n))
                        return (r0 + r) % 2

                    def max_pass(k, h, c):
                        kk = k % (2 * GROUPS)
                        s = fill(("max", k, h, c))
                        max_scores(s, kk // GROUPS, (kk % GROUPS) * GROUP + h, c).then_inc(S["ring_full"], 1)

                    def values(k, half):
                        i = k // GROUPS
                        w = it * (8 * 2 * GROUPS) + (layer * 32 * 2 * GROUPS // 2 + 8 * k + 4 * half + 4 + 2)
                        pe.wait_ge(S["exp_done"], w)
                        for y in range(2):
                            for j in range(GROUP):
                                h = (k % GROUPS) * GROUP + j
                                last = mm(PS[32 * j:32 * j + VW, 6 + k % 2, :], Vs[i][:, 2 * half + y, h, :],
                                          Pb[:, 4 * half + j, y, :], start=(half == 0 and y == 0),
                                          stop=(half == 1 and y == 1))
                        last.then_inc(S["pv_done"], 1)

                    def head_rows(k):
                        s = fill(("oT", k))
                        pe.wait_ge(S["o_read"], it * (2 * GROUPS) + (layer * 4 * GROUPS + k + 1))
                        for c in range(TT):
                            last = nc.tensor.transpose(PS[:, s, c * P:(c + 1) * P], oS[:, k % 2, c * P:(c + 1) * P], ident)
                        last.then_inc(S["ring_full"], 1)

                    def outputs_T(i):
                        s = fill(("OT", i))
                        pe.wait_ge(S["ring_read"], it * DPER + (read0 + DPRO + DVE_READ["oT", GROUPS * (i + 1) - 1]))
                        for c in range(TT):
                            last = nc.tensor.transpose(PS[:, s, c * P:(c + 1) * P], O[:, c, :], ident)
                        last.then_inc(S["ring_full"], 1)

                    def project(i):
                        s = fill(("wo", i))
                        pe.wait_ge(S["ring_read"], it * DPER + (read0 + DPRO + DVE_READ["OT", i]))
                        for c in range(TT):
                            last = mm(PS[:, s, c * P:(c + 1) * P], OT[:, c * P:(c + 1) * P], pr("wo"), start=True, stop=True)
                        last.then_inc(S["ring_full"], 1)

                    for k in range(2 * GROUPS):
                        i = k // GROUPS
                        if k % GROUPS == 0:
                            pe.wait_ge(S[f"v_loaded{i}"], it * 16 + (layer * (3 - i) * 16 + 16))
                        pe.wait_ge(S["max_loaded"], it * (16 * PARTS * 2 * GROUPS) + 16 * PARTS * (splits + 1 + k))
                        for u in range(8):
                            j, half = u % 4, u // 4
                            h = (k % GROUPS) * GROUP + j
                            pe.wait_ge(S["exp_done"], it * (16 * GROUPS) + (layer * 32 * GROUPS + 8 * k + u + 1))
                            for y in range(2):
                                kc = 2 * half + y
                                last = mm(PS[:, 2 + 2 * (u % 2) + y, :], Ks[i][0:SROWS + PARTS, h // 2, kc * P:(kc + 1) * P],
                                          Qs[i][0:SROWS + PARTS, h, :], start=True, stop=True)
                            last.then_inc(S["scores_full"], 1)
                            if k < 2 * GROUPS - 1 or u < 4:
                                if u == 4 and (k + 2) % GROUPS == 0:
                                    nxt = (k + 2) // GROUPS % 2
                                    pe.wait_ge(S[f"qk_loaded{nxt}"],
                                               it * (16 * LDQK) + 16 * LDQK * (layer * (3 - nxt) + 1 + (1 - nxt)))
                                for y in range(2):
                                    max_pass(*lookahead(k, u, y))
                            if u == 1 and k:
                                values(k - 1, 1)
                            if u == 3 and k:
                                head_rows(k - 1)
                            if u == 5:
                                s = fill(("mT", k + 1))
                                pe.wait_ge(S["max_split"], it * (2 * GROUPS) + (splits + 2 + k))
                                max_columns(s, (k + 1) % 2).then_inc(S["ring_full"], 1)
                                values(k, 0)
                            if u == 6 and k == GROUPS:
                                outputs_T(0)
                            if u == 7 and k == GROUPS:
                                project(0)
                    k = 2 * GROUPS - 1
                    for y in range(4):
                        max_pass(k + 2, y // TT, y % TT)
                    values(k, 1)
                    for y in range(4, 8):
                        max_pass(k + 2, y // TT, y % TT)
                    head_rows(k)
                    outputs_T(1)
                    project(1)

            def stage_routing(layer):
                pe.wait_ge(S["rows_ready"], layer * (2 * B + 1) + B + 1)
                for b in range(B):
                    for c in range(TT):
                        last = nc.tensor.transpose(PS[:, b, c * P:(c + 1) * P], N[:, b * TT + c, :], ident)
                    last.then_inc(S["hT_filled"], 1)
                for b in range(B):
                    pe.wait_ge(S["hT2_ready"], layer * B + b + 1)
                    for c in range(TT):
                        last = mm(PS[:, 4, (b * TT + c) * E:(b * TT + c + 1) * E], hT2[:, b, c * P:(c + 1) * P],
                                  pr("gate_w"), start=True, stop=True)
                last.then_inc(S["logits_full"], 1)
                pe.wait_ge(S["hot_ready"], layer + 1)
                flat = hot[:, :, :].rearrange("p t e -> p (t e)")
                mm(PS[:, 5, 0:P], pr("before"), flat, start=True, stop=True)
                mm(PS[:, 5, P:2 * P], pr("ones"), flat, start=True, stop=True).then_inc(S["ranks_full"], 1)

            def stage_experts(layer):
                done = layer * TILES
                with pe.Fori(0, TILES // 2) as it:
                    for i in range(2):
                        pe.wait_ge(S[f"w_loaded{i}"], it * 32 + (layer * TILES // 2 * 32 + 32))
                        nc.tensor.transpose(PS[:, i, 0:P], xt[i][:, :], ident).then_inc(S["xt_full"], 1)
                    for i in range(2):
                        pe.wait_ge(S["xT_ready"], it * 2 + (done + i + 1))
                        for c in range(FC):
                            last = mm(PS[:, 2 + i, c * P:(c + 1) * P], W[i][:, c * P:(c + 1) * P], xT[i][:, :],
                                      start=True, stop=True)
                        last.then_inc(S["mid_full"], 1)
                    for i in range(2):
                        pe.wait_ge(S["mid_ready"], it * 2 + (done + i + 1))
                        for c in range(FC):
                            last = mm(PS[:, 4 + i, 0:P], mid[i][:, c, :], W[i][:, F + c * P:F + (c + 1) * P],
                                      start=(c == 0), stop=(c == FC - 1))
                        last.then_inc(S["y_full"], 1)

            def stage_attention():
                with pe.Fori(0, B) as b:
                    pe.wait_ge(S["attn_done"], b + 1)
                    pe.wait_ge(S["rows_ready"], b + (B + 2))
                    for c in range(TT):
                        last = nc.tensor.transpose(PS[:, 0, c * P:(c + 1) * P], Nb[:, c, :], ident)
                    last.then_inc(S["hT_filled"], 1)
                    pe.wait_ge(S["hT_ready"], b + (1 + B + 1))
                    mm(PS[:, 1, :], pr("aq"), hT[:, :], start=True, stop=True).then_inc(S["a_qkv_full"], 1)
                    mm(PS[:, 2, :], pr("ak"), hT[:, :], start=True, stop=True).then_inc(S["a_qkv_full"], 1)
                    for c in range(TT):
                        last = mm(PS[:, 3, c * P:(c + 1) * P], hT[:, c * P:(c + 1) * P], pr("av"), start=True, stop=True)
                    last.then_inc(S["a_qkv_full"], 1)
                    pe.wait_ge(S["a_qk_read"], b * 2 + 2)
                    pe.wait_ge(S["a_v_read"], b + 1)
                    for c in range(TT):
                        w = (c + 1) * P
                        mm(PS[:, c, 0:w], AT_q[:, c * P:(c + 1) * P], AT_k[:, 0:w], start=True, stop=True).then_inc(S["a_s_full"], 1)
                    for c in range(TT):
                        pe.wait_ge(S["a_exp"], b * TT + (c + 1))
                        if c >= 2:
                            pe.wait_ge(S["a_pT_read"], b * TT + (c - 1))
                        for kc in range(c + 1):
                            last = nc.tensor.transpose(PS[:, 4 + c % 2, kc * P:(kc + 1) * P], AT_p[:, c, kc * P:(kc + 1) * P], ident)
                        last.then_inc(S["a_pT_full"], 1)
                    for c in range(TT):
                        pe.wait_ge(S["a_pT_read"], b * TT + (c + 1))
                        for kc in range(c + 1):
                            last = mm(PS[:, c, 0:P], AT_pT[:, c, kc * P:(kc + 1) * P], AT_v[:, kc, :],
                                      start=(kc == 0), stop=(kc == c))
                        last.then_inc(S["a_o_full"], 1)

            for layer in range(2):
                stage_prep(layer)
                stage_heads(layer)
                stage_routing(layer)
                stage_experts(layer)
                if layer == 0:
                    stage_attention()

        @block.scalar
        def _(act):
            activation = nc.scalar.activation
            act.wait_ge(S["loaded"], 32)
            act.wait_ge(S["setup_done"], 1)

            def stage_prep(layer):
                filled = layer * 3 * B + 1
                with act.Fori(0, B) as b:
                    n = b + (1 + layer * B)
                    act.wait_ge(S["hT_filled"], b + (1 + filled))
                    activation(hT[:, :], PS[:, 0, :], ACT.Identity, bias=pr("b1"), scale=pr("g1")).then_inc(S["hT_ready"], 1)
                    act.wait_ge(S["parts_stored"], n * 32)
                    act.wait_ge(S["rests_ready"], n * 2)
                    for j, bias in ((0, "bq"), (1, "bk")):
                        act.wait_ge(S["qkv_filled"], b * 3 + (layer * 3 * B + 1 + j))
                        activation(full[:, j, :], PS[:, 1 + j, :], ACT.Identity, bias=pr(bias)).then_inc(S["qk_read"], 1)
                        activation(parts[:, j, 0, :], PS[:, 1 + j, :], ACT.Identity, bias=pr(bias)).then_inc(S["qk_read"], 1)
                    for j in range(2):
                        act.wait_ge(S["rests_ready"], n * 2 + (1 + j))
                        activation(parts[:, j, 1, :], rest[:, j, :], ACT.Copy).then_inc(S["mids_ready"], 1)

            def stage_heads(layer):
                start = layer * (PRO + 2 * PER)
                r0 = PRO % 2
                act.wait_ge(S["ring_full"], start + 17)
                activation(MT[:, 0, :], PS[0:PARTS * GROUP, 0, :].bitcast(BF16)[:, 0:T], ACT.Copy).then_inc(S["maxT_ready"], 1)
                with act.Fori(0, 2) as it:
                    def filled(key):
                        act.wait_ge(S["ring_full"], it * PER + (start + PRO + RING[key] + 1))
                        return (r0 + RING[key]) % 2

                    def read_heads(k):
                        act.wait_ge(S["pv_done"], it * (4 * GROUPS) + (layer * 8 * GROUPS + 2 * k + 2 + 2))
                        activation(oS[:, k % 2, :], PS[:, 6 + k % 2, :], ACT.Copy).then_inc(S["o_read"], 1)

                    for k in range(2 * GROUPS):
                        for u in range(8):
                            half = u // 4
                            act.wait_ge(S["scores_full"], it * (16 * GROUPS) + (layer * 32 * GROUPS + 8 * k + u + 1))
                            if u % 4 == 0:
                                act.wait_ge(S["pv_done"], it * (4 * GROUPS) + (layer * 8 * GROUPS + 2 * k + half + 1))
                            activation(Pb[:, u, :, :], PS[:, 2 + 2 * (u % 2):4 + 2 * (u % 2), :], ACT.Exp,
                                       scale=float(HD) ** -0.5).then_inc(S["exp_done"], 1)
                            if u == 2 and k:
                                read_heads(k - 1)
                            if u == 6:
                                s = filled(("mT", k + 1))
                                activation(MT[:, (k + 1) % 2, :], PS[0:PARTS * GROUP, s, :].bitcast(BF16)[:, 0:T],
                                           ACT.Copy).then_inc(S["maxT_ready"], 1)
                    read_heads(2 * GROUPS - 1)

            def stage_routing(layer):
                for b in range(B):
                    act.wait_ge(S["hT_filled"], layer * (3 * B) + B + b + 2)
                    activation(hT2[:, b, :], PS[:, b, :], ACT.Identity, bias=pr("b2"), scale=pr("g2")).then_inc(S["hT2_ready"], 1)

            def stage_experts(layer):
                done = layer * TILES
                with act.Fori(0, TILES // 2) as it:
                    for i in range(2):
                        act.wait_ge(S["mid_full"], it * 2 + (done + i + 1))
                        for c in range(FC):
                            last = activation(mid[i][:, c, :], PS[:, 2 + i, c * P:(c + 1) * P], ACT.Relu,
                                              bias=W[i][:, 2 * F + c:2 * F + c + 1])
                        last.then_inc(S["mid_ready"], 1)

            def stage_attention():
                with act.Fori(0, B) as b:
                    act.wait_ge(S["hT_filled"], b + (2 * B + 2))
                    activation(hT[:, :], PS[:, 0, :], ACT.Copy).then_inc(S["hT_ready"], 1)
                    for j, dst in ((0, AT_q), (1, AT_k)):
                        act.wait_ge(S["a_qkv_full"], b * 3 + (1 + j))
                        activation(dst, PS[:, 1 + j, :], ACT.Copy).then_inc(S["a_qk_read"], 1)
                    for c in range(TT):
                        w = (c + 1) * P
                        act.wait_ge(S["a_max"], b * TT + (c + 1))
                        activation(AT_p[:, c, 0:w], PS[:, c, 0:w], ACT.Exp, scale=float(P) ** -0.5,
                                   bias=amx[:, c:c + 1], accum_out=asum[:, c:c + 1]).then_inc(S["a_exp"], 1)

            for layer in range(2):
                stage_prep(layer)
                stage_heads(layer)
                stage_routing(layer)
                stage_experts(layer)
                if layer == 0:
                    stage_attention()

        @block.vector
        def _(dve):
            v = nc.vector
            step = Tally(S["dve_step"])
            for i in range(2):
                v.memset(Qs[i][:, :, :], 0.0)
                v.memset(Ks[i][:, :, :], 1.0)
            v.memset(Vall[:, :, :], 1.0)
            v.memset(U[:, :, :], 0.0)
            for k in range(2):
                v.memset(PS[:, 6 + k, :], 0.0)
            dve.wait_ge(S["loaded"], 32)
            link(dve, step, v.tensor_copy(identb[:, :], pr("ident")))
            for name, n in (("pv_done", 2), ("exp_done", 2), ("hT_ready", 1), ("hT_filled", 1), ("qk_read", 4),
                            ("v_read", 1), ("rests_ready", 2), ("attn_done", 1), ("parts_stored", 32),
                            ("y_stored0", 16), ("y_stored1", 16), ("setup_done", 1)):
                dve.sem_inc(S[name], n)

            def statistics(src):
                for t in range(NT):
                    step.add(v.bn_stats(stats[:, t, :], src[:, t, :]))
                dve.wait_ge(step.sem, step.now())
                for t in range(NT):
                    v.bn_aggr(mv[:, t, :], stats[:, t, :]).then_inc(S["stat_done"], 1)

            stat = {"n": 0}

            def deviations(src):
                statistics(src)
                stat["n"] += 1
                dve.wait_ge(S["stat_done"], NT * stat["n"])
                dve.wait_ge(S["rstd_ready"], stat["n"])

            def row(t, a):
                return a[:, t, :].rearrange("p o d -> p (o d)")

            def normalise(dst, src):
                deviations(src)
                with dve.Fori(0, B) as b:
                    for c in range(TT):
                        t = bass.ds(b * TT + c, 1)
                        v.tensor_scalar(row(t, dst), row(t, src), row(t, mv)[:, 0:1], row(t, rstd),
                                        ALU.subtract, ALU.mult).then_inc(S["dve_step"], 1)
                step.n += NT
                dve.wait_ge(S["dve_step"], step.n)

            def batch_rows(b, src, turned):
                dve.wait_ge(S["hT_filled"], turned)
                for c in range(TT):
                    t = bass.ds(b * TT + c, 1)
                    last = v.tensor_scalar(Nb[:, c, :], row(t, src), row(t, mv)[:, 0:1], row(t, rstd), ALU.subtract, ALU.mult)
                last.then_inc(S["rows_ready"], 1)

            def stage_prep(layer):
                if layer == 0:
                    dve.wait_ge(S["zeroed"], 32)
                normalise(U, X)
                deviations(U)
                with dve.Fori(0, B) as b:
                    batch_rows(b, U, b + (layer * 3 * B + 1))
                    dve.wait_ge(S["qkv_filled"], b * 3 + (layer * 3 * B + 3))
                    Vb = Vall[:, bass.ds(b, 1), :].rearrange("p o (c h w) -> p (o c) h w", h=NH, w=VW)
                    v.tensor_tensor(Vb[:, :, :, 0:HD], PS[:, 3, :].rearrange("p (c h d) -> p c h d", c=TT, d=HD),
                                    pr("bv").rearrange("p (h d) -> p h d", d=HD).unsqueeze(1).to_broadcast([P, TT, NH, HD]),
                                    ALU.add).then_inc(S["v_read"], 1)
                    for j in range(2):
                        dve.wait_ge(S["qk_read"], b * 4 + (layer * 4 * B + 4 + 2 * j + 2))
                        v.tensor_tensor(rest[:, j, :], full[:, j, :], parts[:, j, 0, :], ALU.subtract).then_inc(S["rests_ready"], 1)
                    for j in range(2):
                        dve.wait_ge(S["mids_ready"], b * 2 + (layer * 2 * B + 1 + j))
                        v.tensor_tensor(parts[:, j, 2, :], rest[:, j, :], parts[:, j, 1, :], ALU.subtract).then_inc(S["parts_ready"], 1)
                    dve.wait_ge(S["parts_ready"], b * 2 + (layer * 2 * B + 2))

            def stage_heads(layer):
                start = layer * (PRO + 2 * PER)
                read0 = layer * (DPRO + 2 * DPER)

                def row_max(slot_, buf, h, c):
                    v.tensor_reduce(M[:, buf, c, h:h + 1], PS[:, slot_, :], AX.X, ALU.max, negate=True).then_inc(S["ring_read"], 1)

                def split_max(buf, ring_read):
                    m = M[:, buf, :, :]
                    dve.wait_ge(S["ring_read"], ring_read)
                    link(dve, step, v.tensor_copy(Mp[:, buf, :, 0, :], m))
                    link(dve, step, v.tensor_tensor(Mr[:, :, :], m, Mp[:, buf, :, 0, :], ALU.subtract))
                    link(dve, step, v.tensor_copy(Mp[:, buf, :, 1, :], Mr[:, :, :]))
                    v.tensor_tensor(Mp[:, buf, :, 2, :], Mr[:, :, :], Mp[:, buf, :, 1, :], ALU.subtract).then_inc(S["max_split"], 1)

                for e in range(16):
                    dve.wait_ge(S["ring_full"], start + e + 1)
                    row_max(e % 2, 0, e // TT, e % TT)
                split_max(0, read0 + 16)
                for e in range(8):
                    dve.wait_ge(S["ring_full"], start + 17 + e + 1)
                    row_max((17 + e) % 2, 1, e // TT, e % TT)

                with dve.Fori(0, 2) as it:
                    step.enter(it, 2 * GROUPS * (3 + 1) + 2)

                    def filled(key):
                        dve.wait_ge(S["ring_full"], it * PER + (start + PRO + RING[key] + 1))
                        return (PRO + RING[key]) % 2

                    def max_pass(k, h, c):
                        row_max(filled(("max", k, h, c)), k % 2, h, c)

                    def normalise_heads(k):
                        s = filled(("oT", k))
                        bank = PS[:, s, :].rearrange("p (c j w) -> p c j w", c=TT, j=GROUP)
                        link(dve, step, v.reciprocal(rden[:, :, :, :], bank[:, :, :, HD:HD + 1]))
                        h0 = (k % GROUPS) * GROUP * HD
                        v.tensor_tensor(O[:, :, h0:h0 + GROUP * HD].rearrange("p c (j d) -> p c j d", d=HD),
                                        bank[:, :, :, 0:HD], rden[:, :, :, :].to_broadcast([P, TT, GROUP, HD]),
                                        ALU.mult).then_inc(S["ring_read"], 1)

                    def outputs_T(i):
                        s = filled(("OT", i))
                        v.tensor_copy(OT[:, :], PS[:, s, :]).then_inc(S["ring_read"], 1)

                    def project(i):
                        s = filled(("wo", i))
                        Ub = U[:, bass.ds((it * 2 + i) * TT, TT), :]
                        bo = pr("bo").unsqueeze(1).to_broadcast([P, TT, P])
                        v.tensor_tensor(tmp[:, :, :], PS[:, s, :].rearrange("p (c d) -> p c d", d=P), bo, ALU.add)\
                            .then_inc(S["ring_read"], 1)
                        dve.wait_ge(S["ring_read"], it * DPER + (read0 + DPRO + DVE_READ["wo", i]))
                        link(dve, step, v.tensor_tensor(Ub, Ub, tmp[:, :, :], ALU.add))

                    for k in range(2 * GROUPS):
                        for u in range(8):
                            if k < 2 * GROUPS - 1 or u < 4:
                                for y in range(2):
                                    max_pass(*lookahead(k, u, y))
                            if u == 3:
                                last = lookahead(k, 3, 1)
                                split_max((k + 1) % 2, it * DPER + (read0 + DPRO + DVE_READ[("max",) + last]))
                                if k:
                                    normalise_heads(k - 1)
                            if u == 6 and k == GROUPS:
                                outputs_T(0)
                            if u == 7 and k == GROUPS:
                                project(0)
                    k = 2 * GROUPS - 1
                    for y in range(8):
                        max_pass(k + 2, y // TT, y % TT)
                    normalise_heads(k)
                    outputs_T(1)
                    project(1)
                step.leave(2)

            def stage_routing(layer):
                dve.wait_ge(S["ring_read"], (layer + 1) * (DPRO + 2 * DPER))
                normalise(N, U)
                dve.sem_inc(S["rows_ready"], 1)
                dve.wait_ge(S["logits_full"], layer + 1)
                gb = pr("gate_b").unsqueeze(1).to_broadcast([P, NT, E])
                io = pr("iota").unsqueeze(1).to_broadcast([P, NT, E])
                link(dve, step, v.tensor_tensor(L[:, :, :], PS[:, 4, 0:NT * E].rearrange("p (t e) -> p t e", e=E), gb, ALU.add))
                link(dve, step, v.tensor_reduce(mx[:, :, 0], L[:, :, :], AX.X, ALU.max))
                link(dve, step, v.tensor_tensor(L2[:, :, :], L[:, :, :], mx[:, :, :].to_broadcast([P, NT, E]), ALU.is_equal))
                link(dve, step, v.tensor_tensor(L[:, :, :], L2[:, :, :], io, ALU.mult))
                link(dve, step, v.tensor_reduce(mx[:, :, 0], L[:, :, :], AX.X, ALU.min))
                v.tensor_tensor(hot[:, :, :], io, mx[:, :, :].to_broadcast([P, NT, E]), ALU.is_equal).then_inc(S["hot_ready"], 1)
                dve.wait_ge(S["ranks_full"], layer + 1)
                tot = PS[:, 5, P:2 * P].rearrange("p (t e) -> p t e", e=E)
                rank = PS[:, 5, 0:P].rearrange("p (t e) -> p t e", e=E)
                link(dve, step, v.tensor_copy(cumA[:, :, :], tot))
                src, dst, d = cumA, cumB, 1
                while d < NT:
                    step.add(v.tensor_copy(dst[:, 0:d, :], src[:, 0:d, :]))
                    link(dve, step, v.tensor_tensor(dst[:, d:NT, :], src[:, d:NT, :], src[:, 0:NT - d, :], ALU.add))
                    src, dst, d = dst, src, 2 * d
                link(dve, step, v.tensor_scalar(nt[:, :], src[:, NT - 1, :], float(P - 1), 1.0 / P, ALU.add, ALU.mult))
                link(dve, step, v.tensor_scalar(nti[:, :], nt[:, :], -0.498, None, ALU.add))
                link(dve, step, v.tensor_copy(nt[:, :], nti[:, :]))
                link(dve, step, v.tensor_copy(ends[:, 0, :], nt[:, :]))
                a, z, d = 0, 1, 1
                while d < E:
                    step.add(v.tensor_copy(ends[:, z, 0:d], ends[:, a, 0:d]))
                    link(dve, step, v.tensor_tensor(ends[:, z, d:E], ends[:, a, d:E], ends[:, a, 0:E - d], ALU.add))
                    a, z, d = z, a, 2 * d
                link(dve, step, v.tensor_tensor(owner[:, :, :], pr("tile").unsqueeze(2).to_broadcast([P, 24, E]),
                                                ends[:, a, :].unsqueeze(1).to_broadcast([P, 24, E]), ALU.is_ge))
                link(dve, step, v.tensor_reduce(ownf[:, :], owner[:, :, :], AX.X, ALU.add))
                link(dve, step, v.tensor_scalar(owni[:, :], ownf[:, :], float(E - 1), None, ALU.min))
                link(dve, step, v.tensor_tensor(nt[:, :], ends[:, a, :], nt[:, :], ALU.subtract))
                link(dve, step, v.tensor_scalar(nt[:, :], nt[:, :], float(P), None, ALU.mult))
                link(dve, step, v.tensor_tensor(src[:, :, :], src[:, :, :], tot, ALU.subtract))
                link(dve, step, v.tensor_tensor(src[:, :, :], src[:, :, :], rank, ALU.add))
                link(dve, step, v.tensor_tensor(src[:, :, :], src[:, :, :], nt[:, :].unsqueeze(1).to_broadcast([P, NT, E]), ALU.add))
                link(dve, step, v.tensor_tensor(src[:, :, :], src[:, :, :], hot[:, :, :], ALU.mult))
                link(dve, step, v.tensor_reduce(slotf[:, :], src[:, :, :], AX.X, ALU.add))
                v.tensor_copy(slot[:, :], slotf[:, :]).then_inc(S["slots_ready"], 1)

            def stage_experts(layer):
                done = layer * TILES
                with dve.Fori(0, TILES // 2) as it:
                    for i in range(2):
                        dve.wait_ge(S["xt_full"], it * 2 + (done + i + 1))
                        v.tensor_scalar(xT[i][:, :], PS[:, i, 0:P], pr("g2"), pr("b2"), ALU.mult, ALU.add).then_inc(S["xT_ready"], 1)
                    for i in range(2):
                        dve.wait_ge(S["y_full"], it * 2 + (done + i + 1))
                        dve.wait_ge(S[f"y_stored{i}"], it * 16 + (layer * TILES // 2 * 16 + 16))
                        v.tensor_tensor(yt[i][:, :], PS[:, 4 + i, 0:P], W[i][:, 2 * F + FC:EW], ALU.add).then_inc(S["y_ready"], 1)
                dve.wait_ge(S["gathered"], 16 * NT * (layer + 1))
                for b in range(B):
                    t = slice(b * TT, (b + 1) * TT)
                    link(dve, step, v.tensor_tensor(U[:, t, :], U[:, t, :], Y[:, t, :], ALU.add))
                    v.scalar_tensor_tensor(X[:, t, :].rearrange("p t d -> p (t d)"), U[:, t, :].rearrange("p t d -> p (t d)"), 0.5,
                                           X[:, t, :].rearrange("p t d -> p (t d)"), ALU.mult, ALU.add).then_inc(S["ffn_done"], 1)
                dve.wait_ge(S["ffn_done"], 4 * (layer + 1))

            def stage_attention():
                deviations(X)
                with dve.Fori(0, B) as b:
                    step.enter(b, 2 * TT + 2 * TT)
                    batch_rows(b, X, b + (2 * B + 1))
                    dve.wait_ge(S["a_qkv_full"], b * 3 + 3)
                    v.tensor_copy(AT_v, PS[:, 3, :].rearrange("p (c d) -> p c d", d=P)).then_inc(S["a_v_read"], 1)
                    for c in range(TT):
                        w = (c + 1) * P
                        dve.wait_ge(S["a_s_full"], b * TT + (c + 1))
                        link(dve, step, v.tensor_tensor(PS[:, c, w - P:w], PS[:, c, w - P:w], pr("causal"), ALU.add))
                        link(dve, step, v.tensor_reduce(arec[:, c:c + 1], PS[:, c, 0:w], AX.X, ALU.max, negate=True))
                        v.tensor_scalar(amx[:, c:c + 1], arec[:, c:c + 1], float(P) ** -0.5, None, ALU.mult).then_inc(S["a_max"], 1)
                    for c in range(TT):
                        w = (c + 1) * P
                        dve.wait_ge(S["a_pT_full"], b * TT + (c + 1))
                        v.tensor_copy(AT_pT[:, c, 0:w], PS[:, 4 + c % 2, 0:w]).then_inc(S["a_pT_read"], 1)
                    for c in range(TT):
                        dve.wait_ge(S["a_o_full"], b * TT + (c + 1))
                        link(dve, step, v.reciprocal(arec[:, c:c + 1], asum[:, c:c + 1]))
                        Xt = X[:, bass.ds(b * TT + c, 1), :].rearrange("p o d -> p (o d)")
                        link(dve, step, v.scalar_tensor_tensor(Xt, PS[:, c, 0:P], arec[:, c:c + 1], Xt, ALU.mult, ALU.add))
                    dve.sem_inc(S["attn_done"], 1)
                step.leave(B)

            for layer in range(2):
                stage_prep(layer)
                stage_heads(layer)
                stage_routing(layer)
                stage_experts(layer)
                if layer == 0:
                    stage_attention()


def kernel(**inputs):
    import concourse.bacc as bacc
    from concourse.bass_utils import run_bass_kernel_spmd as run

    a = {k.removeprefix("L0_"): np.asarray(v) for k, v in inputs.items()}
    cols = {n: np.zeros((P, hi - lo), np.float32) for n, (lo, hi) in _AT.items()}
    for n in ("wq", "wk", "wv", "wo", "gate_w"):
        cols[n] = a["ffn_" + n]
    for n, m in (("aq", "attn_Wq"), ("ak", "attn_Wk"), ("av", "attn_Wv")):
        cols[n] = a[m]
    for n in ("bv", "bo", "gate_b"):
        cols[n] = np.broadcast_to(a["ffn_" + n][None, :], cols[n].shape)
    for n, m in (("g1", "ln1_g"), ("b1", "ln1_b"), ("g2", "ln2_g"), ("b2", "ln2_b"), ("bq", "bq"), ("bk", "bk")):
        cols[n] = a["ffn_" + m][:, None]
    i, j = np.arange(P)[:, None], np.arange(P)[None, :]
    cols["ident"] = (i == j).astype(np.float32)
    cols["before"] = (i < j).astype(np.float32)
    cols["ones"] = np.ones((P, P), np.float32)
    cols["causal"] = np.where(j <= i, 0.0, -3e38).astype(np.float32)
    cols["iota"] = np.broadcast_to(np.arange(E, dtype=np.float32)[None, :] - E, (P, E))
    cols["tile"] = np.broadcast_to(np.arange(24, dtype=np.float32)[None, :], (P, 24))
    params = np.ascontiguousarray(np.concatenate([cols[n] for n in _AT], axis=1))
    experts = np.ascontiguousarray(np.concatenate([
        a["ffn_w1"],
        a["ffn_w2"].reshape(E, FC, P, P).transpose(0, 2, 1, 3).reshape(E, P, FC * P),
        a["ffn_b1"].reshape(E, FC, P).transpose(0, 2, 1),
        np.broadcast_to(a["ffn_b2"][:, None, :], (E, P, P)),
    ], axis=2))
    arrays = {"x": np.ascontiguousarray(a["attn_x"].reshape(B * T, P)), "params": params, "experts": experts}

    nc = bacc.Bacc("TRN2", target_bir_lowering=False, num_devices=1)
    aps = [nc.dram_tensor(n, v.shape, F32, kind="ExternalInput").ap() for n, v in arrays.items()]
    out = nc.dram_tensor("out", (B * T, P), F32, kind="ExternalOutput").ap()
    program(nc, *aps, out)
    r = run(nc, [arrays], core_ids=[0])
    return r.results[0]["out"].reshape(B, T, P)
```

```python
from contextlib import ExitStack

import numpy as np

import concourse.bass as bass
from concourse import mybir

F32 = mybir.dt.float32
BF16 = mybir.dt.bfloat16
I32 = mybir.dt.int32
U32 = mybir.dt.uint32
ALU = mybir.AluOpType
ACT = mybir.ActivationFunctionType
AX = mybir.AxisListType

P = 128
B, T = 4, 512
TT = T // P
NT = B * TT
NH, HD = 16, 8
E, F = 8, 512
FC = F // P
EPS = 1e-5
GROUP = 4
GROUPS = NH // GROUP
PARTS = 3
Q_PART = (0, 0, 1, 1, 0, 2)
K_PART = (0, 1, 0, 1, 2, 0)
STACK = len(Q_PART) * HD
SROWS = 2 * STACK
VW = HD + 1
TILES = NT + E - 1
TILES += TILES % 2
LDQK = 4
STORED = 2 * len(Q_PART) * 16

_AT, _W = {}, 0
for _name, _n in (("ident", P), ("wq", P), ("wk", P), ("wv", P), ("wo", P), ("aq", P), ("ak", P), ("av", P),
                  ("bv", P), ("bo", P), ("causal", P), ("before", P), ("ones", P), ("gate_w", E), ("gate_b", E),
                  ("g1", 1), ("b1", 1), ("g2", 1), ("b2", 1), ("bq", 1), ("bk", 1), ("iota", E), ("tile", 24)):
    _AT[_name] = (_W, _W + _n)
    _W += _n
PARAMS = _W
DEEP = 6
HALF = DEEP // 2
EW = F + FC * P + FC + P


class Tally:

    def __init__(self, sem):
        self.sem, self.n, self.base, self.per = sem, 0, None, 0

    def add(self, ins, by=1):
        ins.then_inc(self.sem, by)
        self.n += by
        return ins

    def now(self):
        return self.n if self.base is None else self.base + self.n

    def enter(self, i, per):
        self.base, self.per, self.start = i * per, per, self.n

    def leave(self, rounds):
        assert self.n - self.start == self.per, (self.n - self.start, self.per)
        self.n = self.start + rounds * self.per
        self.base = None


def ring_entries():
    order = {}

    def put(*key):
        order[key] = len(order)

    for k in range(2 * GROUPS):
        for u in range(8):
            if not at_end(k, u):
                for y in range(2):
                    put("max", *lookahead(k, u, y))
            if u == 3:
                put("mT", k + 1)
            if u == 4 and k:
                put("oT", k - 1)
            if u == 6 and k == GROUPS:
                put("OT", 0)
            if u == 7 and k == GROUPS:
                put("wo", 0)
    for u in LATE:
        for y in range(2):
            put("max", *lookahead(k, u, y))
    put("oT", k)
    put("OT", 1)
    put("wo", 1)
    return order


def lookahead(k, u, y):
    e = 2 * u + y
    return k + 2, e // TT, e % TT


LATE = (6, 7)


def at_end(k, u):
    return k == 2 * GROUPS - 1 and u in LATE


RING = ring_entries()
PER = len(RING)
RING_BANKS = (0, 1, 7)
PRO = 16 + 1 + 16
ORDER = list(RING)
DVE_READ = {key: sum(o[0] != "mT" for o in ORDER[:r + 1]) for key, r in RING.items()}
DPER = PER - 2 * GROUPS
DPRO = PRO - 1


def program(nc, x, params, experts, out):
    with ExitStack() as ctx:
        def sb(name, shape, dt=F32):
            return ctx.enter_context(nc.sbuf_tensor(name, shape, dt))

        def sem(name):
            return ctx.enter_context(nc.semaphore(name))

        q_dram = nc.dram_tensor("q_stacks", (B, NH, STACK, T), BF16).ap()
        k_dram = nc.dram_tensor("k_stacks", (B, NH, STACK, T), BF16).ap()
        xs_dram = nc.dram_tensor("sorted_in", (TILES * P, P), F32).ap()
        ys_dram = nc.dram_tensor("sorted_out", (TILES * P, P), F32).ap()

        par = sb("par", [P, PARAMS])
        X = sb("X", [P, NT, P])
        U = sb("U", [P, NT, P])
        N = sb("N", [P, NT, P])
        Nb = sb("Nb", [P, TT, P])
        Y = sb("Y", [P, NT, P])
        stats = sb("stats", [P, NT, 6])
        mv = sb("mv", [P, NT, 2])
        rstd = sb("rstd", [P, NT, 1])
        nhalf = sb("nhalf", [P, NT])
        hT = sb("hT", [P, T])
        full = sb("full", [P, 2, T])
        rest = sb("rest", [P, 2, T])
        parts = sb("parts", [P, 2, PARTS, T], BF16)
        Vall = sb("Vall", [P, B, TT * NH * VW])
        Qs = [sb(f"Qs{i}", [P, NH, T], BF16) for i in range(2)]
        Ks = [sb(f"Ks{i}", [P, NH // 2, T], BF16) for i in range(2)]
        Vs = [sb(f"Vs{i}", [P, TT, NH, VW]) for i in range(2)]
        M = sb("M", [P, 2, TT, GROUP])
        Mr = sb("Mr", [P, TT, GROUP])
        zero = sb("zero", [P, TT, GROUP])
        Mp = sb("Mp", [P, 2, TT, PARTS, GROUP], BF16)
        MT = sb("MT", [PARTS * GROUP, 2, T], BF16)
        Pb = sb("Pb", [P, 8, 2, T])
        oS = sb("oS", [P, 2, T])
        rden = sb("rden", [P, TT, GROUP, 1])
        O = sb("O", [P, TT, P])
        OT = sb("OT", [P, T])
        tmp = sb("tmp", [P, TT, P])
        yt = sb("yt", [P, DEEP, P])
        xt = sb("xt", [P, DEEP, P])
        xT = [sb(f"xT{i}", [P, P]) for i in range(2)]
        mid = [sb(f"mid{i}", [P, FC, P]) for i in range(2)]
        identb = sb("identb", [P, P], BF16)
        L = sb("L", [P, NT, E])
        L2 = sb("L2", [P, NT, E])
        mx = sb("mx", [P, NT, 1])
        hot = sb("hot", [P, NT, E])
        cumA = sb("cumA", [P, NT, E])
        cumB = sb("cumB", [P, NT, E])
        nt = sb("nt", [P, E])
        nti = sb("nti", [P, E], I32)
        ends = sb("ends", [P, 2, E])
        slotf = sb("slotf", [P, NT])
        slot = sb("slot", [P, NT], U32)
        owner = sb("owner", [P, 24, E])
        ownf = sb("ownf", [P, 24])
        owni = sb("owni", [P, 24], I32)
        AT_p = Pb[:, 0:2, :, :].rearrange("p a b t -> p (a b) t")
        AT_pT = Pb[:, 2:4, :, :].rearrange("p a b t -> p (a b) t")
        AT_q, AT_k = Pb[:, 4, 0, :], Pb[:, 4, 1, :]
        AT_v = Pb[:, 5, 0, :].rearrange("p (c d) -> p c d", d=P)
        hT2 = Pb[:, 6:8, :, :].rearrange("p a b t -> p (a b) t")
        flat = Pb[:, :, :, :].rearrange("p a b t -> p (a b t)")
        W = [flat[:, i * EW:(i + 1) * EW] for i in range(DEEP)]
        amx = sb("amx", [P, TT])
        asum = sb("asum", [P, TT])
        arec = sb("arec", [P, TT])
        PS = ctx.enter_context(nc.psum_tensor("PS", [P, 8, T], F32))

        def pr(name, rows=P):
            a, b = _AT[name]
            return par[0:rows, a:b]

        S = {n: sem(n) for n in (
            "loaded", "x_stored", "zeros_ready", "zeroed", "stacks_clear", "setup_done", "dve_step", "pool_step",
            "stat_done", "rstd_ready", "rows_ready",
            "hT_filled", "hT_ready", "qkv_filled", "v_read", "qk_read", "mids_ready", "rests_ready", "parts_ready",
            "parts_stored", "qk_loaded0", "qk_loaded1", "v_loaded0", "v_loaded1",
            "ring_full", "ring_read", "maxT_ready", "max_split", "max_loaded",
            "scores_full", "exp_done", "pv_done", "o_read",
            "hT2_ready", "logits_full", "hot_ready", "ranks_full", "slots_ready", "scattered",
            "w_loaded0", "w_loaded1", "w_loaded2", "w_loaded3", "w_loaded4", "w_loaded5", "xt_loaded0", "xt_loaded1", "xt_full", "xT_ready", "mid_full", "mid_ready", "y_full", "y_ready",
            "y_stored0", "y_stored1", "gathered", "ffn_done",
            "a_qkv_full", "a_qk_read", "a_v_read", "a_s_full", "a_max", "a_exp", "a_pT_full", "a_pT_read",
            "a_o_full", "attn_done")}

        def link(eng, tally, ins):
            tally.add(ins)
            eng.wait_ge(tally.sem, tally.now())

        def ring_bank(n):
            return RING_BANKS[n % 3]

        block = ctx.enter_context(nc.Block())

        @block.sync
        def _(sp):
            sp.dma_start(par[:, :], params).then_inc(S["loaded"], 16)
            sp.dma_start(X[:, :, :], x.rearrange("(t p) d -> p t d", p=P)).then_inc(S["loaded"], 16)
            sp.wait_ge(S["zeros_ready"], 1)
            sp.dma_start(xs_dram.rearrange("(j p) d -> p j d", p=P)[:, 0:12, :], N[:, 0:12, :]).then_inc(S["zeroed"], 16)
            sp.dma_start(xs_dram.rearrange("(j p) d -> p j d", p=P)[:, 12:24, :], N[:, 0:12, :]).then_inc(S["zeroed"], 16)

            def load_stacks(i, b):
                for r in range(2):
                    for src, to in ((q_dram, Qs[i][r * STACK:(r + 1) * STACK, r::2, :]), (k_dram, Ks[i][r * STACK:(r + 1) * STACK, :, :])):
                        v = src[bass.ds(b, 1), :, :, :].rearrange("o (s r) m t -> m s (o r) t", r=2)[:, :, r, :]
                        sp.dma_start(to, v).then_inc(S[f"qk_loaded{i}"], 16)
                sp.dma_start(Vs[i][:, :, :, :].rearrange("p c h w -> p (c h w)"),
                             Vall[:, bass.ds(b, 1), :].rearrange("p o w -> p (o w)")).then_inc(S[f"v_loaded{i}"], 16)

            def load_max(n, buf, i, h0):
                sp.wait_ge(S["maxT_ready"], n)
                for p in range(PARTS):
                    sp.dma_start(Qs[i][SROWS + p:SROWS + p + 1, h0:h0 + GROUP, :],
                                 MT[p * GROUP:(p + 1) * GROUP, buf, :]).then_inc(S["max_loaded"], 16)

            def load_weights(j, i, through=None):
                e = sp.value_load(owni[0:1, bass.ds(j, 1)], min_val=0, max_val=E - 1)
                if through is not None:
                    sp.wait_ge(S["y_ready"], through)
                sp.dma_start(W[i], experts[bass.ds(e, 1), :, :].rearrange("o p w -> p (o w)")).then_inc(S[f"w_loaded{i}"], 16)

            def rows_of(dram, j):
                return dram[bass.ds(j * (HALF * P), HALF * P), :].rearrange("(i p) d -> p i d", p=P)

            def load_rows(j, half):
                sp.dma_start(xt[:, half * HALF:(half + 1) * HALF, :], rows_of(xs_dram, j)).then_inc(S[f"xt_loaded{half}"], 16)

            def store_rows(j, half):
                sp.dma_start(rows_of(ys_dram, j), yt[:, half * HALF:(half + 1) * HALF, :]).then_inc(S[f"y_stored{half}"], 16)

            for layer in range(2):
                with sp.Fori(0, B) as b:
                    sp.wait_ge(S["parts_ready"], b * 2 + (2 + layer * 2 * B))
                    for j, dst, pick in ((0, q_dram, Q_PART), (1, k_dram, K_PART)):
                        for g, part in enumerate(pick):
                            to = dst[bass.ds(b, 1), :, g * HD:(g + 1) * HD, :].rearrange("o h d t -> (o h) d t")
                            sp.dma_start(to, parts[:, j, part, :]).then_inc(S["parts_stored"], 16)
                sp.wait_ge(S["parts_stored"], STORED * (B * (layer + 1) + 1))
                sp.wait_ge(S["v_read"], B * (layer + 1) + 1)
                if layer == 0:
                    sp.wait_ge(S["stacks_clear"], 1)
                else:
                    sp.wait_ge(S["ring_full"], layer * (PRO + 2 * PER))
                load_stacks(0, 0)
                mt = layer * (1 + 2 * 2 * GROUPS)
                load_max(mt + 1, 0, 0, 0)
                with sp.Fori(0, 2) as it:
                    for k in range(2 * GROUPS):
                        if k == 0:
                            sp.wait_ge(S["pv_done"], it * (4 * GROUPS) + (2 + layer * 8 * GROUPS))
                            load_stacks(1, it * 2 + 1)
                        if k == GROUPS:
                            sp.wait_ge(S["pv_done"], it * (4 * GROUPS) + (2 + 2 * GROUPS + layer * 8 * GROUPS))
                            load_stacks(0, it * (-2) + 2)
                        kk = k + 1
                        load_max(it * (2 * GROUPS) + (mt + 1 + kk), kk % 2, (kk // GROUPS) % 2, (kk % GROUPS) * GROUP)
                sp.wait_ge(S["max_loaded"], 16 * PARTS * (1 + 4 * GROUPS) * (layer + 1))
                sp.wait_ge(S["slots_ready"], layer + 1)
                sp.wait_ge(S["scattered"], 16 * NT * (layer + 1))
                for half in range(2):
                    load_rows(half, half)
                    for i in range(half * HALF, (half + 1) * HALF):
                        load_weights(i, i)
                rounds = TILES // DEEP
                with sp.Fori(0, rounds - 1) as it:
                    for half in range(2):
                        for i in range(half * HALF, (half + 1) * HALF):
                            load_weights(it * DEEP + (DEEP + i), i, it * DEEP + (2 + layer * TILES + i + 1))
                        store_rows(it * 2 + half, half)
                        load_rows(it * 2 + (2 + half), half)
                for half in range(2):
                    sp.wait_ge(S["y_ready"], 2 + layer * TILES + TILES - DEEP + HALF * (half + 1))
                    store_rows((rounds - 1) * 2 + half, half)

            sp.wait_ge(S["ffn_done"], 2 * 4)
            sp.dma_start(out.rearrange("(t p) d -> p t d", p=P), X[:, :, :]).then_inc(S["x_stored"], 16)
            sp.wait_ge(S["x_stored"], 16)

        @block.gpsimd
        def _(pool):
            step = Tally(S["pool_step"])
            link(pool, step, nc.gpsimd.memset(nhalf[:, :], -0.5))
            link(pool, step, nc.gpsimd.memset(zero[:, :, :], 0.0))
            link(pool, step, nc.gpsimd.memset(N[:, :, :], 0.0))
            pool.sem_inc(S["zeros_ready"], 1)
            for i in range(2):
                link(pool, step, nc.gpsimd.memset(Qs[i][:, :, :].bitcast(F32), 0.0))
            link(pool, step, nc.gpsimd.memset(Vall[:, :, :], 1.0))
            pool.sem_inc(S["stacks_clear"], 1)

            def inverse_deviations(n):
                pool.wait_ge(S["stat_done"], NT * n)
                link(pool, step, nc.gpsimd.tensor_scalar(rstd[:, :, 0], mv[:, :, 1], EPS, 1.0, ALU.add, ALU.mult))
                nc.gpsimd.tensor_tensor(rstd[:, :, 0], rstd[:, :, 0], nhalf[:, :], ALU.pow).then_inc(S["rstd_ready"], 1)

            def split_max(buf, ring_read):
                m, part = M[:, buf, :, :], Mp[:, buf, :, :, :]
                pool.wait_ge(S["ring_read"], ring_read)
                link(pool, step, nc.gpsimd.tensor_tensor(part[:, :, 0, :], m, zero[:, :, :], ALU.add))
                link(pool, step, nc.gpsimd.tensor_tensor(Mr[:, :, :], m, part[:, :, 0, :], ALU.subtract))
                link(pool, step, nc.gpsimd.tensor_tensor(part[:, :, 1, :], Mr[:, :, :], zero[:, :, :], ALU.add))
                nc.gpsimd.tensor_tensor(part[:, :, 2, :], Mr[:, :, :], part[:, :, 1, :], ALU.subtract).then_inc(S["max_split"], 1)

            n = 0
            for layer in range(2):
                for _ in range(2):
                    n += 1
                    inverse_deviations(n)
                read0 = layer * (DPRO + 2 * DPER)
                split_max(0, read0 + 16)
                with pool.Fori(0, 2) as it:
                    step.enter(it, 2 * GROUPS * 3)
                    for k in range(2 * GROUPS):
                        n_read = DVE_READ[("max",) + lookahead(k - 1, 7, 1)] if k else 0
                        split_max((k + 1) % 2, it * DPER + (read0 + DPRO + n_read))
                step.leave(2)
                n += 1
                inverse_deviations(n)
                pool.wait_ge(S["zeroed"], 32)
                pool.wait_ge(S["slots_ready"], layer + 1)
                for t in range(NT):
                    nc.gpsimd.indirect_dma_start(xs_dram, bass.IndirectOffsetOnAxis(slot[:, t:t + 1], 0),
                                                 N[:, t, :], None).then_inc(S["scattered"], 16)
                for i in range(2):
                    pool.wait_ge(S[f"y_stored{i}"], 16 * (TILES // DEEP * (layer + 1) + 1))
                for t in range(NT):
                    nc.gpsimd.indirect_dma_start(Y[:, t, :], None, ys_dram,
                                                 bass.IndirectOffsetOnAxis(slot[:, t:t + 1], 0)).then_inc(S["gathered"], 16)
                if layer == 0:
                    n += 1
                    inverse_deviations(n)

        @block.tensor
        def _(pe):
            ident = pr("ident")
            mm = nc.tensor.matmul
            pe.wait_ge(S["loaded"], 32)
            pe.wait_ge(S["setup_done"], 1)

            def stage_prep(layer):
                with pe.Fori(0, B) as b:
                    n = b + (1 + layer * B)
                    turned = b + (1 + layer * 2 * B)
                    pe.wait_ge(S["hT_ready"], turned)
                    pe.wait_ge(S["rows_ready"], b + (layer * (2 * B + 1) + 1))
                    for c in range(TT):
                        last = nc.tensor.transpose(PS[:, 0, c * P:(c + 1) * P], Nb[:, c, :], ident)
                    last.then_inc(S["hT_filled"], 1)
                    pe.wait_ge(S["hT_ready"], turned + 1)
                    pe.wait_ge(S["qk_read"], n * 4)
                    mm(PS[:, 1, :], pr("wq"), hT[:, :], start=True, stop=True).then_inc(S["qkv_filled"], 1)
                    mm(PS[:, 2, :], pr("wk"), hT[:, :], start=True, stop=True).then_inc(S["qkv_filled"], 1)
                    pe.wait_ge(S["v_read"], n)
                    for c in range(TT):
                        last = mm(PS[:, 3, c * P:(c + 1) * P], hT[:, c * P:(c + 1) * P], pr("wv"), start=True, stop=True)
                    last.then_inc(S["qkv_filled"], 1)

            def max_scores(slot_, i, h, c):
                return mm(PS[:, slot_, :], Qs[i][0:SROWS, h, c * P:(c + 1) * P], Ks[i][0:SROWS, h // 2, :],
                          start=True, stop=True)

            def max_columns(slot_, buf):
                bank = PS[0:PARTS * GROUP, slot_, :].bitcast(BF16)
                for c in range(TT):
                    last = nc.tensor.transpose(bank[:, c * P:(c + 1) * P],
                                               Mp[:, buf, c, :, :].rearrange("p a j -> p (a j)"), identb[:, :])
                return last

            def stage_heads(layer):
                start = layer * (PRO + 2 * PER)
                splits = layer * (1 + 2 * 2 * GROUPS)
                read0 = layer * (DPRO + 2 * DPER)

                pe.wait_ge(S["qk_loaded0"], layer * 3 * 16 * LDQK + 16 * LDQK)
                for e in range(16):
                    if e >= 3:
                        pe.wait_ge(S["ring_read"], read0 + e - 2)
                    max_scores(ring_bank(e), 0, e // TT, e % TT).then_inc(S["ring_full"], 1)
                pe.wait_ge(S["ring_read"], read0 + 14)
                pe.wait_ge(S["max_split"], splits + 1)
                max_columns(ring_bank(16), 0).then_inc(S["ring_full"], 1)
                for e in range(16):
                    if e == 2:
                        pe.wait_ge(S["maxT_ready"], splits + 1)
                    else:
                        pe.wait_ge(S["ring_read"], read0 + 15 + e if e < 2 else read0 + 14 + e)
                    max_scores(ring_bank(17 + e), 0, GROUP + e // TT, e % TT).then_inc(S["ring_full"], 1)

                with pe.Fori(0, 2) as it:
                    def fill(key):
                        r = RING[key]
                        before = ORDER[r - 3]
                        if r >= 3 and before[0] == "mT":
                            pe.wait_ge(S["maxT_ready"], it * (2 * GROUPS) + (splits + 1 + before[1]))
                        else:
                            n = DVE_READ[before] if r >= 3 else 0
                            pe.wait_ge(S["ring_read"], it * DPER + (read0 + DPRO + n))
                        return ring_bank(PRO + r)

                    def max_pass(k, h, c):
                        kk = k % (2 * GROUPS)
                        s = fill(("max", k, h, c))
                        max_scores(s, kk // GROUPS, (kk % GROUPS) * GROUP + h, c).then_inc(S["ring_full"], 1)

                    def values(k, kc):
                        i, half, y = k // GROUPS, kc // 2, kc % 2
                        w = it * (8 * 2 * GROUPS) + (layer * 32 * 2 * GROUPS // 2 + 8 * k + 4 * half + 4 + 2)
                        pe.wait_ge(S["exp_done"], w)
                        for j in range(GROUP):
                            h = (k % GROUPS) * GROUP + j
                            last = mm(PS[32 * j:32 * j + VW, 6, :], Vs[i][:, kc, h, :],
                                      Pb[:, 4 * half + j, y, :], start=(kc == 0), stop=(kc == TT - 1))
                        if y == 1:
                            last.then_inc(S["pv_done"], 1)

                    def head_rows(k):
                        s = fill(("oT", k))
                        pe.wait_ge(S["o_read"], it * (2 * GROUPS) + (layer * 4 * GROUPS + k + 1))
                        for c in range(TT):
                            last = nc.tensor.transpose(PS[:, s, c * P:(c + 1) * P], oS[:, k % 2, c * P:(c + 1) * P], ident)
                        last.then_inc(S["ring_full"], 1)

                    def outputs_T(i):
                        s = fill(("OT", i))
                        pe.wait_ge(S["ring_read"], it * DPER + (read0 + DPRO + DVE_READ["oT", GROUPS * (i + 1) - 1]))
                        for c in range(TT):
                            last = nc.tensor.transpose(PS[:, s, c * P:(c + 1) * P], O[:, c, :], ident)
                        last.then_inc(S["ring_full"], 1)

                    def project(i):
                        s = fill(("wo", i))
                        pe.wait_ge(S["ring_read"], it * DPER + (read0 + DPRO + DVE_READ["OT", i]))
                        for c in range(TT):
                            last = mm(PS[:, s, c * P:(c + 1) * P], OT[:, c * P:(c + 1) * P], pr("wo"), start=True, stop=True)
                        last.then_inc(S["ring_full"], 1)

                    for k in range(2 * GROUPS):
                        i = k // GROUPS
                        if k % GROUPS == 0:
                            pe.wait_ge(S[f"v_loaded{i}"], it * 16 + (layer * (3 - i) * 16 + 16))
                        pe.wait_ge(S["max_loaded"], it * (16 * PARTS * 2 * GROUPS) + 16 * PARTS * (splits + 1 + k))
                        for u in range(8):
                            j, half = u % 4, u // 4
                            h = (k % GROUPS) * GROUP + j
                            pe.wait_ge(S["exp_done"], it * (16 * GROUPS) + (layer * 32 * GROUPS + 8 * k + u + 1))
                            for y in range(2):
                                kc = 2 * half + y
                                last = mm(PS[:, 2 + 2 * (u % 2) + y, :], Ks[i][0:SROWS + PARTS, h // 2, kc * P:(kc + 1) * P],
                                          Qs[i][0:SROWS + PARTS, h, :], start=True, stop=True)
                            last.then_inc(S["scores_full"], 1)
                            if not at_end(k, u):
                                if u == 0 and (k + 2) % GROUPS == 0:
                                    nxt = (k + 2) // GROUPS % 2
                                    pe.wait_ge(S[f"qk_loaded{nxt}"],
                                               it * (16 * LDQK) + 16 * LDQK * (layer * (3 - nxt) + 1 + (1 - nxt)))
                                for y in range(2):
                                    max_pass(*lookahead(k, u, y))
                            if u in (1, 2) and k:
                                values(k - 1, u + 1)
                            if u == 3:
                                s = fill(("mT", k + 1))
                                pe.wait_ge(S["max_split"], it * (2 * GROUPS) + (splits + 2 + k))
                                max_columns(s, (k + 1) % 2).then_inc(S["ring_full"], 1)
                            if u == 4 and k:
                                head_rows(k - 1)
                            if u in (5, 6):
                                values(k, u - 5)
                            if u == 6 and k == GROUPS:
                                outputs_T(0)
                            if u == 7 and k == GROUPS:
                                project(0)
                    for u in LATE:
                        for y in range(2):
                            max_pass(*lookahead(k, u, y))
                    values(k, 2)
                    values(k, 3)
                    head_rows(k)
                    outputs_T(1)
                    project(1)

            def stage_routing(layer):
                pe.wait_ge(S["rows_ready"], layer * (2 * B + 1) + B + 1)
                for b in range(B):
                    for c in range(TT):
                        last = nc.tensor.transpose(PS[:, b, c * P:(c + 1) * P], N[:, b * TT + c, :], ident)
                    last.then_inc(S["hT_filled"], 1)
                for b in range(B):
                    pe.wait_ge(S["hT2_ready"], layer * B + b + 1)
                    for c in range(TT):
                        last = mm(PS[:, 4, (b * TT + c) * E:(b * TT + c + 1) * E], hT2[:, b, c * P:(c + 1) * P],
                                  pr("gate_w"), start=True, stop=True)
                last.then_inc(S["logits_full"], 1)
                pe.wait_ge(S["hot_ready"], layer + 1)
                flat = hot[:, :, :].rearrange("p t e -> p (t e)")
                mm(PS[:, 5, 0:P], pr("before"), flat, start=True, stop=True)
                mm(PS[:, 5, P:2 * P], pr("ones"), flat, start=True, stop=True).then_inc(S["ranks_full"], 1)

            def stage_experts(layer):
                done, rounds = layer * TILES, TILES // DEEP
                with pe.Fori(0, rounds) as it:
                    def turn(i):
                        if i % HALF == 0:
                            pe.wait_ge(S[f"xt_loaded{i // HALF}"], it * 16 + (layer * rounds * 16 + 16))
                        nc.tensor.transpose(PS[:, i % 2, 0:P], xt[:, i, :], ident).then_inc(S["xt_full"], 1)

                    def result(i):
                        pe.wait_ge(S["y_ready"], it * DEEP + (done + i + 1))
                        pe.wait_ge(S["mid_ready"], it * DEEP + (done + i + 1))
                        for c in range(FC):
                            last = mm(PS[:, 4 + i % 2, 0:P], mid[i % 2][:, c, :], W[i][:, F + c * P:F + (c + 1) * P],
                                      start=(c == 0), stop=(c == FC - 1))
                        last.then_inc(S["y_full"], 1)

                    turn(0)
                    for i in range(DEEP):
                        if i < DEEP - 1:
                            turn(i + 1)
                        pe.wait_ge(S[f"w_loaded{i}"], it * 16 + (layer * rounds * 16 + 16))
                        pe.wait_ge(S["xT_ready"], it * DEEP + (done + i + 1))
                        for c in range(FC):
                            last = mm(PS[:, 2 + i % 2, c * P:(c + 1) * P], W[i][:, c * P:(c + 1) * P], xT[i % 2][:, :],
                                      start=True, stop=True)
                        last.then_inc(S["mid_full"], 1)
                        if i:
                            result(i - 1)
                    result(DEEP - 1)

            def stage_attention():
                with pe.Fori(0, B) as b:
                    pe.wait_ge(S["attn_done"], b + 1)
                    pe.wait_ge(S["rows_ready"], b + (B + 2))
                    for c in range(TT):
                        last = nc.tensor.transpose(PS[:, 0, c * P:(c + 1) * P], Nb[:, c, :], ident)
                    last.then_inc(S["hT_filled"], 1)
                    pe.wait_ge(S["hT_ready"], b + (1 + B + 1))
                    mm(PS[:, 1, :], pr("aq"), hT[:, :], start=True, stop=True).then_inc(S["a_qkv_full"], 1)
                    mm(PS[:, 2, :], pr("ak"), hT[:, :], start=True, stop=True).then_inc(S["a_qkv_full"], 1)
                    for c in range(TT):
                        last = mm(PS[:, 3, c * P:(c + 1) * P], hT[:, c * P:(c + 1) * P], pr("av"), start=True, stop=True)
                    last.then_inc(S["a_qkv_full"], 1)
                    pe.wait_ge(S["a_qk_read"], b * 2 + 2)
                    pe.wait_ge(S["a_v_read"], b + 1)
                    for c in range(TT):
                        w = (c + 1) * P
                        mm(PS[:, c, 0:w], AT_q[:, c * P:(c + 1) * P], AT_k[:, 0:w], start=True, stop=True).then_inc(S["a_s_full"], 1)
                    for c in range(TT):
                        pe.wait_ge(S["a_exp"], b * TT + (c + 1))
                        if c >= 2:
                            pe.wait_ge(S["a_pT_read"], b * TT + (c - 1))
                        for kc in range(c + 1):
                            last = nc.tensor.transpose(PS[:, 4 + c % 2, kc * P:(kc + 1) * P], AT_p[:, c, kc * P:(kc + 1) * P], ident)
                        last.then_inc(S["a_pT_full"], 1)
                    for c in range(TT):
                        pe.wait_ge(S["a_pT_read"], b * TT + (c + 1))
                        for kc in range(c + 1):
                            last = mm(PS[:, c, 0:P], AT_pT[:, c, kc * P:(kc + 1) * P], AT_v[:, kc, :],
                                      start=(kc == 0), stop=(kc == c))
                        last.then_inc(S["a_o_full"], 1)

            for layer in range(2):
                stage_prep(layer)
                stage_heads(layer)
                stage_routing(layer)
                stage_experts(layer)
                if layer == 0:
                    stage_attention()

        @block.scalar
        def _(act):
            activation = nc.scalar.activation
            act.wait_ge(S["loaded"], 32)
            act.wait_ge(S["setup_done"], 1)

            def stage_prep(layer):
                filled = layer * 3 * B + 1
                with act.Fori(0, B) as b:
                    n = b + (1 + layer * B)
                    act.wait_ge(S["hT_filled"], b + (1 + filled))
                    activation(hT[:, :], PS[:, 0, :], ACT.Identity, bias=pr("b1"), scale=pr("g1")).then_inc(S["hT_ready"], 1)
                    act.wait_ge(S["parts_stored"], n * STORED)
                    act.wait_ge(S["rests_ready"], n * 2)
                    for j, bias in ((0, "bq"), (1, "bk")):
                        act.wait_ge(S["qkv_filled"], b * 3 + (layer * 3 * B + 1 + j))
                        activation(full[:, j, :], PS[:, 1 + j, :], ACT.Identity, bias=pr(bias)).then_inc(S["qk_read"], 1)
                        activation(parts[:, j, 0, :], PS[:, 1 + j, :], ACT.Identity, bias=pr(bias)).then_inc(S["qk_read"], 1)
                    for j in range(2):
                        act.wait_ge(S["rests_ready"], n * 2 + (1 + j))
                        activation(parts[:, j, 1, :], rest[:, j, :], ACT.Copy).then_inc(S["mids_ready"], 1)

            def stage_heads(layer):
                start = layer * (PRO + 2 * PER)
                act.wait_ge(S["ring_full"], start + 17)
                activation(MT[:, 0, :], PS[0:PARTS * GROUP, ring_bank(16), :].bitcast(BF16)[:, 0:T], ACT.Copy).then_inc(S["maxT_ready"], 1)
                with act.Fori(0, 2) as it:
                    def filled(key):
                        act.wait_ge(S["ring_full"], it * PER + (start + PRO + RING[key] + 1))
                        return ring_bank(PRO + RING[key])

                    def read_heads(k):
                        act.wait_ge(S["pv_done"], it * (4 * GROUPS) + (layer * 8 * GROUPS + 2 * k + 2 + 2))
                        activation(oS[:, k % 2, :], PS[:, 6, :], ACT.Copy).then_inc(S["o_read"], 1)

                    for k in range(2 * GROUPS):
                        for u in range(8):
                            half = u // 4
                            act.wait_ge(S["scores_full"], it * (16 * GROUPS) + (layer * 32 * GROUPS + 8 * k + u + 1))
                            if u % 4 == 0:
                                act.wait_ge(S["pv_done"], it * (4 * GROUPS) + (layer * 8 * GROUPS + 2 * k + half + 1))
                            activation(Pb[:, u, :, :], PS[:, 2 + 2 * (u % 2):4 + 2 * (u % 2), :], ACT.Exp,
                                       scale=float(HD) ** -0.5).then_inc(S["exp_done"], 1)
                            if u == 3 and k:
                                read_heads(k - 1)
                            if u == 4:
                                s = filled(("mT", k + 1))
                                activation(MT[:, (k + 1) % 2, :], PS[0:PARTS * GROUP, s, :].bitcast(BF16)[:, 0:T],
                                           ACT.Copy).then_inc(S["maxT_ready"], 1)
                    read_heads(2 * GROUPS - 1)

            def stage_routing(layer):
                for b in range(B):
                    act.wait_ge(S["hT_filled"], layer * (3 * B) + B + b + 2)
                    activation(hT2[:, b, :], PS[:, b, :], ACT.Identity, bias=pr("b2"), scale=pr("g2")).then_inc(S["hT2_ready"], 1)

            def stage_experts(layer):
                with act.Fori(0, TILES // DEEP) as it:
                    for i in range(DEEP):
                        act.wait_ge(S["mid_full"], it * DEEP + (layer * TILES + i + 1))
                        for c in range(FC):
                            last = activation(mid[i % 2][:, c, :], PS[:, 2 + i % 2, c * P:(c + 1) * P], ACT.Relu,
                                              bias=W[i][:, 2 * F + c:2 * F + c + 1])
                        last.then_inc(S["mid_ready"], 1)

            def stage_attention():
                with act.Fori(0, B) as b:
                    act.wait_ge(S["hT_filled"], b + (2 * B + 2))
                    activation(hT[:, :], PS[:, 0, :], ACT.Copy).then_inc(S["hT_ready"], 1)
                    for j, dst in ((0, AT_q), (1, AT_k)):
                        act.wait_ge(S["a_qkv_full"], b * 3 + (1 + j))
                        activation(dst, PS[:, 1 + j, :], ACT.Copy).then_inc(S["a_qk_read"], 1)
                    for c in range(TT):
                        w = (c + 1) * P
                        act.wait_ge(S["a_max"], b * TT + (c + 1))
                        activation(AT_p[:, c, 0:w], PS[:, c, 0:w], ACT.Exp, scale=float(P) ** -0.5,
                                   bias=amx[:, c:c + 1], accum_out=asum[:, c:c + 1]).then_inc(S["a_exp"], 1)

            for layer in range(2):
                stage_prep(layer)
                stage_heads(layer)
                stage_routing(layer)
                stage_experts(layer)
                if layer == 0:
                    stage_attention()

        @block.vector
        def _(dve):
            v = nc.vector
            step = Tally(S["dve_step"])
            v.memset(PS[:, 6, :], 0.0)
            for i in range(2):
                v.memset(Ks[i][SROWS:P, :, :], 1.0)
            dve.wait_ge(S["loaded"], 32)
            link(dve, step, v.tensor_copy(identb[:, :], pr("ident")))
            for name, n in (("pv_done", 2), ("exp_done", 2), ("y_ready", 2), ("hT_ready", 1), ("hT_filled", 1), ("qk_read", 4),
                            ("v_read", 1), ("rests_ready", 2), ("attn_done", 1), ("parts_stored", STORED),
                            ("y_stored0", 16), ("y_stored1", 16), ("setup_done", 1)):
                dve.sem_inc(S[name], n)

            def statistics(src):
                for t in range(NT):
                    step.add(v.bn_stats(stats[:, t, :], src[:, t, :]))
                dve.wait_ge(step.sem, step.now())
                for t in range(NT):
                    v.bn_aggr(mv[:, t, :], stats[:, t, :]).then_inc(S["stat_done"], 1)

            stat = {"n": 0}

            def deviations(src):
                statistics(src)
                stat["n"] += 1
                dve.wait_ge(S["stat_done"], NT * stat["n"])
                dve.wait_ge(S["rstd_ready"], stat["n"])

            def row(t, a):
                return a[:, t, :].rearrange("p o d -> p (o d)")

            def normalise(dst, src):
                deviations(src)
                for t in range(NT):
                    last = v.tensor_scalar(dst[:, t, :], src[:, t, :], mv[:, t, 0:1], rstd[:, t, :], ALU.subtract, ALU.mult)
                link(dve, step, last)

            def batch_rows(b, src, turned):
                dve.wait_ge(S["hT_filled"], turned)
                for c in range(TT):
                    t = bass.ds(b * TT + c, 1)
                    last = v.tensor_scalar(Nb[:, c, :], row(t, src), row(t, mv)[:, 0:1], row(t, rstd), ALU.subtract, ALU.mult)
                last.then_inc(S["rows_ready"], 1)

            def stage_prep(layer):
                normalise(U, X)
                deviations(U)
                if layer == 0:
                    dve.wait_ge(S["stacks_clear"], 1)
                with dve.Fori(0, B) as b:
                    batch_rows(b, U, b + (layer * 3 * B + 1))
                    dve.wait_ge(S["qkv_filled"], b * 3 + (layer * 3 * B + 3))
                    Vb = Vall[:, bass.ds(b, 1), :].rearrange("p o (c h w) -> p (o c) h w", h=NH, w=VW)
                    v.tensor_tensor(Vb[:, :, :, 0:HD], PS[:, 3, :].rearrange("p (c h d) -> p c h d", c=TT, d=HD),
                                    pr("bv").rearrange("p (h d) -> p h d", d=HD).unsqueeze(1).to_broadcast([P, TT, NH, HD]),
                                    ALU.add).then_inc(S["v_read"], 1)
                    for j in range(2):
                        dve.wait_ge(S["qk_read"], b * 4 + (layer * 4 * B + 4 + 2 * j + 2))
                        v.tensor_tensor(rest[:, j, :], full[:, j, :], parts[:, j, 0, :], ALU.subtract).then_inc(S["rests_ready"], 1)
                    for j in range(2):
                        dve.wait_ge(S["mids_ready"], b * 2 + (layer * 2 * B + 1 + j))
                        v.tensor_tensor(parts[:, j, 2, :], rest[:, j, :], parts[:, j, 1, :], ALU.subtract).then_inc(S["parts_ready"], 1)
                    dve.wait_ge(S["parts_ready"], b * 2 + (layer * 2 * B + 2))

            def stage_heads(layer):
                start = layer * (PRO + 2 * PER)
                read0 = layer * (DPRO + 2 * DPER)

                def row_max(slot_, buf, h, c):
                    v.tensor_reduce(M[:, buf, c, h:h + 1], PS[:, slot_, :], AX.X, ALU.max, negate=True).then_inc(S["ring_read"], 1)

                for e in range(16):
                    dve.wait_ge(S["ring_full"], start + e + 1)
                    row_max(ring_bank(e), 0, e // TT, e % TT)
                for e in range(16):
                    dve.wait_ge(S["ring_full"], start + 17 + e + 1)
                    row_max(ring_bank(17 + e), 1, e // TT, e % TT)

                with dve.Fori(0, 2) as it:
                    step.enter(it, 2 * GROUPS + 2)

                    def filled(key):
                        dve.wait_ge(S["ring_full"], it * PER + (start + PRO + RING[key] + 1))
                        return ring_bank(PRO + RING[key])

                    def max_pass(k, h, c):
                        row_max(filled(("max", k, h, c)), k % 2, h, c)

                    def normalise_heads(k):
                        s = filled(("oT", k))
                        bank = PS[:, s, :].rearrange("p (c j w) -> p c j w", c=TT, j=GROUP)
                        link(dve, step, v.reciprocal(rden[:, :, :, :], bank[:, :, :, HD:HD + 1]))
                        h0 = (k % GROUPS) * GROUP * HD
                        v.tensor_tensor(O[:, :, h0:h0 + GROUP * HD].rearrange("p c (j d) -> p c j d", d=HD),
                                        bank[:, :, :, 0:HD], rden[:, :, :, :].to_broadcast([P, TT, GROUP, HD]),
                                        ALU.mult).then_inc(S["ring_read"], 1)

                    def outputs_T(i):
                        s = filled(("OT", i))
                        v.tensor_copy(OT[:, :], PS[:, s, :]).then_inc(S["ring_read"], 1)

                    def project(i):
                        s = filled(("wo", i))
                        Ub = U[:, bass.ds((it * 2 + i) * TT, TT), :]
                        bo = pr("bo").unsqueeze(1).to_broadcast([P, TT, P])
                        v.tensor_tensor(tmp[:, :, :], PS[:, s, :].rearrange("p (c d) -> p c d", d=P), bo, ALU.add)\
                            .then_inc(S["ring_read"], 1)
                        dve.wait_ge(S["ring_read"], it * DPER + (read0 + DPRO + DVE_READ["wo", i]))
                        link(dve, step, v.tensor_tensor(Ub, Ub, tmp[:, :, :], ALU.add))

                    for k in range(2 * GROUPS):
                        for u in range(8):
                            if not at_end(k, u):
                                for y in range(2):
                                    max_pass(*lookahead(k, u, y))
                            if u == 4 and k:
                                normalise_heads(k - 1)
                            if u == 6 and k == GROUPS:
                                outputs_T(0)
                            if u == 7 and k == GROUPS:
                                project(0)
                    for u in LATE:
                        for y in range(2):
                            max_pass(*lookahead(k, u, y))
                    normalise_heads(k)
                    outputs_T(1)
                    project(1)
                step.leave(2)

            def stage_routing(layer):
                dve.wait_ge(S["ring_read"], (layer + 1) * (DPRO + 2 * DPER))
                if layer == 0:
                    dve.wait_ge(S["zeroed"], 32)
                normalise(N, U)
                dve.sem_inc(S["rows_ready"], 1)
                dve.wait_ge(S["logits_full"], layer + 1)
                gb = pr("gate_b").unsqueeze(1).to_broadcast([P, NT, E])
                io = pr("iota").unsqueeze(1).to_broadcast([P, NT, E])
                link(dve, step, v.tensor_tensor(L[:, :, :], PS[:, 4, 0:NT * E].rearrange("p (t e) -> p t e", e=E), gb, ALU.add))
                link(dve, step, v.tensor_reduce(mx[:, :, 0], L[:, :, :], AX.X, ALU.max))
                link(dve, step, v.tensor_tensor(L2[:, :, :], L[:, :, :], mx[:, :, :].to_broadcast([P, NT, E]), ALU.is_equal))
                link(dve, step, v.tensor_tensor(L[:, :, :], L2[:, :, :], io, ALU.mult))
                link(dve, step, v.tensor_reduce(mx[:, :, 0], L[:, :, :], AX.X, ALU.min))
                v.tensor_tensor(hot[:, :, :], io, mx[:, :, :].to_broadcast([P, NT, E]), ALU.is_equal).then_inc(S["hot_ready"], 1)
                dve.wait_ge(S["ranks_full"], layer + 1)
                tot = PS[:, 5, P:2 * P].rearrange("p (t e) -> p t e", e=E)
                rank = PS[:, 5, 0:P].rearrange("p (t e) -> p t e", e=E)
                link(dve, step, v.tensor_copy(cumA[:, :, :], tot))
                src, dst, d = cumA, cumB, 1
                while d < NT:
                    step.add(v.tensor_copy(dst[:, 0:d, :], src[:, 0:d, :]))
                    link(dve, step, v.tensor_tensor(dst[:, d:NT, :], src[:, d:NT, :], src[:, 0:NT - d, :], ALU.add))
                    src, dst, d = dst, src, 2 * d
                link(dve, step, v.tensor_scalar(nt[:, :], src[:, NT - 1, :], float(P - 1), 1.0 / P, ALU.add, ALU.mult))
                link(dve, step, v.tensor_scalar(nti[:, :], nt[:, :], -0.498, None, ALU.add))
                link(dve, step, v.tensor_copy(nt[:, :], nti[:, :]))
                link(dve, step, v.tensor_copy(ends[:, 0, :], nt[:, :]))
                a, z, d = 0, 1, 1
                while d < E:
                    step.add(v.tensor_copy(ends[:, z, 0:d], ends[:, a, 0:d]))
                    link(dve, step, v.tensor_tensor(ends[:, z, d:E], ends[:, a, d:E], ends[:, a, 0:E - d], ALU.add))
                    a, z, d = z, a, 2 * d
                link(dve, step, v.tensor_tensor(owner[:, :, :], pr("tile").unsqueeze(2).to_broadcast([P, 24, E]),
                                                ends[:, a, :].unsqueeze(1).to_broadcast([P, 24, E]), ALU.is_ge))
                link(dve, step, v.tensor_reduce(ownf[:, :], owner[:, :, :], AX.X, ALU.add))
                link(dve, step, v.tensor_scalar(owni[:, :], ownf[:, :], float(E - 1), None, ALU.min))
                link(dve, step, v.tensor_tensor(nt[:, :], ends[:, a, :], nt[:, :], ALU.subtract))
                link(dve, step, v.tensor_scalar(nt[:, :], nt[:, :], float(P), None, ALU.mult))
                link(dve, step, v.tensor_tensor(src[:, :, :], src[:, :, :], tot, ALU.subtract))
                link(dve, step, v.tensor_tensor(src[:, :, :], src[:, :, :], rank, ALU.add))
                link(dve, step, v.tensor_tensor(src[:, :, :], src[:, :, :], nt[:, :].unsqueeze(1).to_broadcast([P, NT, E]), ALU.add))
                link(dve, step, v.tensor_tensor(src[:, :, :], src[:, :, :], hot[:, :, :], ALU.mult))
                link(dve, step, v.tensor_reduce(slotf[:, :], src[:, :, :], AX.X, ALU.add))
                v.tensor_copy(slot[:, :], slotf[:, :]).then_inc(S["slots_ready"], 1)

            def stage_experts(layer):
                done, rounds = layer * TILES, TILES // DEEP
                with dve.Fori(0, rounds) as it:
                    def turned(i):
                        dve.wait_ge(S["xt_full"], it * DEEP + (done + i + 1))
                        v.tensor_scalar(xT[i % 2][:, :], PS[:, i % 2, 0:P], pr("g2"), pr("b2"), ALU.mult, ALU.add).then_inc(S["xT_ready"], 1)

                    def result(i):
                        if i % HALF == 0:
                            dve.wait_ge(S[f"y_stored{i // HALF}"], it * 16 + (layer * rounds * 16 + 16))
                        dve.wait_ge(S["y_full"], it * DEEP + (done + i + 1))
                        v.tensor_tensor(yt[:, i, :], PS[:, 4 + i % 2, 0:P], W[i][:, 2 * F + FC:EW], ALU.add).then_inc(S["y_ready"], 1)

                    turned(0)
                    for i in range(DEEP):
                        if i < DEEP - 1:
                            turned(i + 1)
                        if i:
                            result(i - 1)
                    result(DEEP - 1)
                dve.wait_ge(S["gathered"], 16 * NT * (layer + 1))
                for b in range(B):
                    t = slice(b * TT, (b + 1) * TT)
                    link(dve, step, v.tensor_tensor(U[:, t, :], U[:, t, :], Y[:, t, :], ALU.add))
                    v.scalar_tensor_tensor(X[:, t, :].rearrange("p t d -> p (t d)"), U[:, t, :].rearrange("p t d -> p (t d)"), 0.5,
                                           X[:, t, :].rearrange("p t d -> p (t d)"), ALU.mult, ALU.add).then_inc(S["ffn_done"], 1)
                dve.wait_ge(S["ffn_done"], 4 * (layer + 1))

            def stage_attention():
                deviations(X)
                with dve.Fori(0, B) as b:
                    step.enter(b, 2 * TT + 2 * TT)
                    batch_rows(b, X, b + (2 * B + 1))
                    dve.wait_ge(S["a_qkv_full"], b * 3 + 3)
                    v.tensor_copy(AT_v, PS[:, 3, :].rearrange("p (c d) -> p c d", d=P)).then_inc(S["a_v_read"], 1)
                    for c in range(TT):
                        w = (c + 1) * P
                        dve.wait_ge(S["a_s_full"], b * TT + (c + 1))
                        link(dve, step, v.tensor_tensor(PS[:, c, w - P:w], PS[:, c, w - P:w], pr("causal"), ALU.add))
                        link(dve, step, v.tensor_reduce(arec[:, c:c + 1], PS[:, c, 0:w], AX.X, ALU.max, negate=True))
                        v.tensor_scalar(amx[:, c:c + 1], arec[:, c:c + 1], float(P) ** -0.5, None, ALU.mult).then_inc(S["a_max"], 1)
                    for c in range(TT):
                        w = (c + 1) * P
                        dve.wait_ge(S["a_pT_full"], b * TT + (c + 1))
                        v.tensor_copy(AT_pT[:, c, 0:w], PS[:, 4 + c % 2, 0:w]).then_inc(S["a_pT_read"], 1)
                    for c in range(TT):
                        dve.wait_ge(S["a_o_full"], b * TT + (c + 1))
                        link(dve, step, v.reciprocal(arec[:, c:c + 1], asum[:, c:c + 1]))
                        Xt = X[:, bass.ds(b * TT + c, 1), :].rearrange("p o d -> p (o d)")
                        link(dve, step, v.scalar_tensor_tensor(Xt, PS[:, c, 0:P], arec[:, c:c + 1], Xt, ALU.mult, ALU.add))
                    dve.sem_inc(S["attn_done"], 1)
                step.leave(B)

            for layer in range(2):
                stage_prep(layer)
                stage_heads(layer)
                stage_routing(layer)
                stage_experts(layer)
                if layer == 0:
                    stage_attention()


def kernel(**inputs):
    import concourse.bacc as bacc
    from concourse.bass_utils import run_bass_kernel_spmd as run

    a = {k.removeprefix("L0_"): np.asarray(v) for k, v in inputs.items()}
    cols = {n: np.zeros((P, hi - lo), np.float32) for n, (lo, hi) in _AT.items()}
    for n in ("wq", "wk", "wv", "wo", "gate_w"):
        cols[n] = a["ffn_" + n]
    for n, m in (("aq", "attn_Wq"), ("ak", "attn_Wk"), ("av", "attn_Wv")):
        cols[n] = a[m]
    for n in ("bv", "bo", "gate_b"):
        cols[n] = np.broadcast_to(a["ffn_" + n][None, :], cols[n].shape)
    for n, m in (("g1", "ln1_g"), ("b1", "ln1_b"), ("g2", "ln2_g"), ("b2", "ln2_b"), ("bq", "bq"), ("bk", "bk")):
        cols[n] = a["ffn_" + m][:, None]
    i, j = np.arange(P)[:, None], np.arange(P)[None, :]
    cols["ident"] = (i == j).astype(np.float32)
    cols["before"] = (i < j).astype(np.float32)
    cols["ones"] = np.ones((P, P), np.float32)
    cols["causal"] = np.where(j <= i, 0.0, -3e38).astype(np.float32)
    cols["iota"] = np.broadcast_to(np.arange(E, dtype=np.float32)[None, :] - E, (P, E))
    cols["tile"] = np.broadcast_to(np.arange(24, dtype=np.float32)[None, :], (P, 24))
    params = np.ascontiguousarray(np.concatenate([cols[n] for n in _AT], axis=1))
    experts = np.ascontiguousarray(np.concatenate([
        a["ffn_w1"],
        a["ffn_w2"].reshape(E, FC, P, P).transpose(0, 2, 1, 3).reshape(E, P, FC * P),
        a["ffn_b1"].reshape(E, FC, P).transpose(0, 2, 1),
        np.broadcast_to(a["ffn_b2"][:, None, :], (E, P, P)),
    ], axis=2))
    arrays = {"x": np.ascontiguousarray(a["attn_x"].reshape(B * T, P)), "params": params, "experts": experts}

    nc = bacc.Bacc("TRN2", target_bir_lowering=False, num_devices=1)
    aps = [nc.dram_tensor(n, v.shape, F32, kind="ExternalInput").ap() for n, v in arrays.items()]
    out = nc.dram_tensor("out", (B * T, P), F32, kind="ExternalOutput").ap()
    program(nc, *aps, out)
    r = run(nc, [arrays], core_ids=[0])
    return r.results[0]["out"].reshape(B, T, P)
```

```python
from contextlib import ExitStack

import numpy as np

import concourse.bass as bass
from concourse import mybir

F32 = mybir.dt.float32
BF16 = mybir.dt.bfloat16
I32 = mybir.dt.int32
U32 = mybir.dt.uint32
ALU = mybir.AluOpType
ACT = mybir.ActivationFunctionType
AX = mybir.AxisListType

P = 128
B, T = 4, 512
TT = T // P
NT = B * TT
NH, HD = 16, 8
E, F = 8, 512
FC = F // P
EPS = 1e-5
GROUP = 4
GROUPS = NH // GROUP
PARTS = 3
Q_PART = (0, 0, 0, 1, 1, 2)
RUNS = ((0, 3), (3, 2), (5, 1))
STACK = len(Q_PART) * HD
SROWS = 2 * STACK
VW = HD + 1
TILES = NT + E - 1
COLS = TILES + TILES % 2
LDQK = 4
STORED = 2 * len(RUNS) * 16

_AT, _W = {}, 0
for _name, _n in (("ident", P), ("wq", P), ("wk", P), ("wv", P), ("wo", P), ("aq", P), ("ak", P), ("av", P),
                  ("bv", P), ("bo", P), ("causal", P), ("before", P), ("ones", P), ("gate_w", E), ("gate_b", E),
                  ("g1", 1), ("b1", 1), ("g2", 1), ("b2", 1), ("bq", 1), ("bk", 1), ("iota", E), ("tile", COLS),
                  ("place", P), ("back", NT), ("row", 1), ("slot", COLS), ("first", E * E)):
    _AT[_name] = (_W, _W + _n)
    _W += _n
PARAMS = _W
DEEP = 6
SUMS = (2, 7)
LOOPS, REST = divmod(TILES - 1, DEEP)
BEHIND = 3
EW = F + FC * P + FC + P


PREP_ORDER = ((("x", 0), ("x", 1), ("u", 0), ("x", 2), ("u", 1), ("x", 3), ("u", 2), ("u", 3)),
              (("x", 0), ("u", 0), ("x", 1), ("u", 1), ("x", 2), ("x", 3), ("u", 2), ("u", 3)))
NEXT = {(2, 2): 0, (3, 0): 1, (3, 2): 2, (3, 3): 3, (4, 2): 4}
PREPARED = len(NEXT)


def stat_number(layer, rows, b):
    n = layer * 4 * B + 1
    if rows in ("x", "u"):
        return n + PREP_ORDER[layer].index((rows, b))
    return n + {"ffn": 2, "attn": 3}[rows] * B + b


def uses(i):
    return len(range(i % DEEP, TILES, DEEP))


def filled_by(layer, it, i):
    return it * 16 + 16 * (layer * uses(i) + i // DEEP + 1)


class Tally:

    def __init__(self, sem):
        self.sem, self.n, self.base, self.per = sem, 0, None, 0

    def add(self, ins, by=1):
        ins.then_inc(self.sem, by)
        self.n += by
        return ins

    def now(self):
        return self.n if self.base is None else self.base + self.n

    def enter(self, i, per):
        self.base, self.per, self.start = i * per, per, self.n

    def leave(self, rounds):
        assert self.n - self.start == self.per, (self.n - self.start, self.per)
        self.n = self.start + rounds * self.per
        self.base = None


def ring_entries():
    order, late = {}, 0

    def put(*key):
        order[key] = len(order)

    for k in range(2 * GROUPS):
        for u in range(8):
            if not at_end(k, u):
                for y in range(2):
                    put("max", *lookahead(k, u, y))
            if u == 3:
                put("mT", k + 1)
            if u == 4 and k:
                put("oT", k - 1)
            if u == 7 and k == GROUPS:
                put("OT", 0)
            if u == 0 and k == GROUPS + 1:
                put("wo", 0)
    for what in TAIL:
        if what == "max":
            put("max", *lookahead(k, LATE[late // 2], late % 2))
            late += 1
        elif what == "oT":
            put("oT", k)
        elif what in ("OT", "wo"):
            put(what, 1)
    return order


def lookahead(k, u, y):
    e = 2 * u + y
    return k + 2, e // TT, e % TT


LATE = (6, 7)
TAIL = ("values", "max", "values", "max", "oT", "max", "OT", "max", "wo")


def at_end(k, u):
    return k == 2 * GROUPS - 1 and u in LATE


RING = ring_entries()
PER = len(RING)
RING_BANKS = (0, 1, 7)
PRO = 16 + 1 + 16
ORDER = list(RING)
DVE_READ = {key: sum(o[0] != "mT" for o in ORDER[:r + 1]) for key, r in RING.items()}
DPER = PER - 2 * GROUPS
DPRO = PRO - 1


def program(nc, x, params, experts, out):
    with ExitStack() as ctx:
        def sb(name, shape, dt=F32):
            return ctx.enter_context(nc.sbuf_tensor(name, shape, dt))

        def sem(name):
            return ctx.enter_context(nc.semaphore(name))

        q_dram = nc.dram_tensor("q_stacks", (B, NH, STACK, T), BF16).ap()
        k_dram = nc.dram_tensor("k_stacks", (B, NH, STACK, T), BF16).ap()
        n_dram = nc.dram_tensor("expert_in", (NT * P, P), F32).ap()
        y_dram = nc.dram_tensor("expert_out", ((NT + COLS) * P, P), F32).ap()

        par = sb("par", [P, PARAMS])
        X = sb("X", [P, NT, P])
        U = sb("U", [P, NT, P])
        N = sb("N", [P, NT, P])
        Nb = sb("Nb", [P, 2, TT, P])
        Y = sb("Y", [P, NT, P])
        stats = sb("stats", [P, NT, 6])
        mv = sb("mv", [P, NT, 2])
        rstd = sb("rstd", [P, NT, 1])
        nhalf = sb("nhalf", [P, NT])
        shift = sb("shift", [P, NT])
        hT = sb("hT", [P, 2, T])
        rest = sb("rest", [P, 2, 2, T])
        parts = sb("parts", [P, 2, 2, PARTS, T], BF16)
        Vall = sb("Vall", [P, B, TT * NH * VW])
        Qs = [sb(f"Qs{i}", [P, NH, T], BF16) for i in range(2)]
        Ks = [sb(f"Ks{i}", [P, NH // 2, T], BF16) for i in range(2)]
        Vs = [sb(f"Vs{i}", [P, TT, NH, VW]) for i in range(2)]
        M = sb("M", [P, 2, TT, GROUP])
        Mr = sb("Mr", [P, TT, GROUP])
        zero = sb("zero", [P, TT, GROUP])
        Mp = sb("Mp", [P, 2, TT, PARTS, GROUP], BF16)
        MT = sb("MT", [PARTS * GROUP, 2, T], BF16)
        Pb = sb("Pb", [P, 8, 2, T])
        oS = sb("oS", [P, 2, T])
        rden = sb("rden", [P, TT, GROUP, 1])
        O = sb("O", [P, TT, P])
        OT = sb("OT", [P, T])
        tmp = sb("tmp", [P, TT, P])
        yt = sb("yt", [P, DEEP, P])
        xt = sb("xt", [P, DEEP, P])
        xT = [sb(f"xT{i}", [P, P]) for i in range(2)]
        mid = [sb(f"mid{i}", [P, FC, P]) for i in range(2)]
        identb = sb("identb", [P, P], BF16)
        onesb = sb("onesb", [PARTS, T], BF16)
        beforeb = sb("beforeb", [P, P], BF16)
        allb = sb("allb", [P, P], BF16)
        gateW = sb("gateW", [P, E])
        gateC = sb("gateC", [P, 1, E])
        gateB = sb("gateB", [P, 1, E])
        L = sb("L", [P, NT, E])
        L2 = sb("L2", [P, NT, E])
        mx = sb("mx", [P, NT, 1])
        hot = sb("hot", [P, NT + 1, E], BF16)
        src = sb("src", [P, NT, E])
        nt = sb("nt", [P, E])
        nti = sb("nti", [P, E], I32)
        lowers = sb("lowers", [P, E, E])
        first = sb("first", [P, E])
        slotf = sb("slotf", [P, NT])
        tilei = sb("tilei", [P, NT], I32)
        tilef = sb("tilef", [P, NT, 1])
        placef = sb("placef", [P, NT, 1])
        isTile = sb("isTile", [P, NT, COLS], BF16)
        inTile = sb("inTile", [P, NT, 2, COLS], BF16)
        atPlace = sb("atPlace", [P, NT, P], BF16)
        toks = sb("toks", [P, COLS])
        tok_in = sb("tok_in", [P, COLS], U32)
        tok_out = sb("tok_out", [P, COLS], U32)
        owner = sb("owner", [P, COLS, E])
        ownf = sb("ownf", [P, COLS])
        owni = sb("owni", [P, COLS], I32)
        flat = Pb[:, :, :, :].rearrange("p a b t -> p (a b t)")
        W = [flat[:, i * EW:(i + 1) * EW] for i in range(DEEP)]
        AT_p = [flat[:, i * TT * T:(i + 1) * TT * T].rearrange("p (c t) -> p c t", t=T) for i in range(2)]
        AT_pT, AT_q, AT_k = ([flat[:, i * T:(i + 1) * T] for i in (a, a + 1)] for a in (8, 10, 12))
        AT_v = [N[:, b * TT:(b + 1) * TT, :].rearrange("p t d -> p (t d)") for b in range(B)]
        hT2 = Pb[:, 6:8, :, :].rearrange("p a b t -> p (a b) t")
        amx = sb("amx", [P, 2, TT])
        asum = sb("asum", [P, B, TT])
        arec = sb("arec", [P, TT, 1])
        PS = ctx.enter_context(nc.psum_tensor("PS", [P, 8, T], F32))

        def pr(name, rows=P):
            a, b = _AT[name]
            return par[0:rows, a:b]

        S = {n: sem(n) for n in (
            "x_loaded0", "x_loaded1", "x_loaded2", "x_loaded3", "loaded", "x_stored",
            "q_clear", "v_ones", "ones_ready", "k_ones", "setup_done", "dve_step", "pool_step",
            "stat_done", "rstd_ready", "rows_ready", "hT_filled", "hT_ready", "qkv_filled", "v_read",
            "firsts_ready", "rests_ready", "mids_ready", "q_parts", "k_parts", "parts_stored0", "parts_stored1",
            "qk_loaded0", "qk_loaded1", "v_loaded0", "v_loaded1",
            "ring_full", "ring_read", "maxT_ready", "max_split", "max_loaded",
            "scores_full", "exp_done", "pv_done", "o_read",
            "gates_ready", "gates_full", "gates_read", "u_ready", "n_ready", "hT2_filled", "hT2_ready", "logits_full", "hot_ready", "ranks_full", "owners_ready", "tiles_ready", "places_ready",
            "pool_places", "tokens_full", "tokens_ready", "n_stored",
            "w_loaded0", "w_loaded1", "w_loaded2", "w_loaded3", "w_loaded4", "w_loaded5", "xt_loaded0", "xt_loaded1", "xt_loaded2", "xt_loaded3", "xt_loaded4", "xt_loaded5", "xt_full", "xT_ready", "mid_full", "mid_ready", "y_full", "y_ready",
            "y_stored0", "y_stored1", "y_stored2", "y_stored3", "y_stored4", "y_stored5", "yt_free",
            "y_loaded0", "y_loaded1", "y_loaded2", "y_loaded3", "ffn_done",
            "a_rows", "a_hT_filled", "a_hT_ready", "a_qkv_full", "a_qk_read", "a_v_read", "a_s_full", "a_max", "a_exp",
            "a_pT_full", "a_pT_read", "a_pT3_read", "a_o_full", "a_o_read")}

        def link(eng, tally, ins):
            tally.add(ins)
            eng.wait_ge(tally.sem, tally.now())

        def ring_bank(n):
            return RING_BANKS[n % 3]

        block = ctx.enter_context(nc.Block())

        @block.sync
        def _(sp):
            def load_x(b):
                sp.dma_start(X[:, b * TT:(b + 1) * TT, :],
                             x[b * T:(b + 1) * T, :].rearrange("(t p) d -> p t d", p=P)).then_inc(S[f"x_loaded{b}"], 16)

            load_x(0)
            sp.dma_start(par[:, :], params).then_inc(S["loaded"], 16)
            for b in range(1, B):
                load_x(b)
            sp.wait_ge(S["ones_ready"], 1)
            for i in range(2):
                sp.dma_start(Ks[i][SROWS:SROWS + PARTS, :, :],
                             onesb[0:PARTS, :].unsqueeze(1).to_broadcast([PARTS, NH // 2, T])).then_inc(S["k_ones"], 16)

            def load_stacks(i, b):
                for r in range(2):
                    for src, to in ((q_dram, Qs[i][r * STACK:(r + 1) * STACK, r::2, :]), (k_dram, Ks[i][r * STACK:(r + 1) * STACK, :, :])):
                        v = src[bass.ds(b, 1), :, :, :].rearrange("o (s r) m t -> m s (o r) t", r=2)[:, :, r, :]
                        sp.dma_start(to, v).then_inc(S[f"qk_loaded{i}"], 16)
                sp.dma_start(Vs[i][:, :, :, :].rearrange("p c h w -> p (c h w)"),
                             Vall[:, bass.ds(b, 1), :].rearrange("p o w -> p (o w)")).then_inc(S[f"v_loaded{i}"], 16)

            def load_max(n, buf, i, h0):
                sp.wait_ge(S["maxT_ready"], n)
                for p in range(PARTS):
                    sp.dma_start(Qs[i][SROWS + p:SROWS + p + 1, h0:h0 + GROUP, :],
                                 MT[p * GROUP:(p + 1) * GROUP, buf, :]).then_inc(S["max_loaded"], 16)

            def load_weights(j, i, through=None):
                e = sp.value_load(owni[0:1, bass.ds(j, 1)], min_val=0, max_val=E - 1)
                if through is not None:
                    sp.wait_ge(S["y_ready"], through)
                sp.dma_start(W[i], experts[bass.ds(e, 1), :, :].rearrange("o p w -> p (o w)")).then_inc(S[f"w_loaded{i}"], 16)

            for layer in range(2):
                for b in range(B):
                    n = layer * B + b
                    for part in range(PARTS):
                        for j, dst in ((0, q_dram), (1, k_dram)):
                            if part < 2:
                                sp.wait_ge(S[("firsts_ready", "mids_ready")[part]], 2 * n + 1 + j)
                            else:
                                sp.wait_ge(S[("q_parts", "k_parts")[j]], n + 1)
                            g, count = RUNS[part if j == 0 else PARTS - 1 - part]
                            to = dst[b, :, :, :].rearrange("h (d g) t -> (h d) g t", d=HD)[:, g:g + count, :]
                            src = parts[:, b % 2, j, Q_PART[g]:Q_PART[g] + 1, :].to_broadcast([P, count, T]) if j == 0 else \
                                parts[:, b % 2, j, 0:count, :]
                            sp.dma_start(to, src).then_inc(S[f"parts_stored{b % 2}"], 16)
                    if b == 0:
                        sp.wait_ge(S["parts_stored0"], STORED * (2 * layer + 1))
                        sp.wait_ge(S["v_read"], layer * B + 1)
                        if layer == 0:
                            sp.wait_ge(S["q_clear"], 1)
                        else:
                            sp.wait_ge(S["ring_full"], layer * (PRO + 2 * PER))
                        load_stacks(0, 0)
                for i in range(2):
                    sp.wait_ge(S[f"parts_stored{i}"], STORED * 2 * (layer + 1))
                sp.wait_ge(S["v_read"], B * (layer + 1))
                mt = layer * (1 + 2 * 2 * GROUPS)
                load_max(mt + 1, 0, 0, 0)
                if layer == 0:
                    sp.wait_ge(S["q_clear"], 2)
                with sp.Fori(0, 2) as it:
                    for k in range(2 * GROUPS):
                        if k == 0:
                            sp.wait_ge(S["pv_done"], it * (4 * GROUPS) + (2 + layer * 8 * GROUPS))
                            load_stacks(1, it * 2 + 1)
                        if k == GROUPS:
                            sp.wait_ge(S["pv_done"], it * (4 * GROUPS) + (2 + 2 * GROUPS + layer * 8 * GROUPS))
                            load_stacks(0, it * (-2) + 2)
                        kk = k + 1
                        load_max(it * (2 * GROUPS) + (mt + 1 + kk), kk % 2, (kk // GROUPS) % 2, (kk % GROUPS) * GROUP)
                sp.wait_ge(S["max_loaded"], 16 * PARTS * (1 + 4 * GROUPS) * (layer + 1))
                for b in range(B):
                    sp.wait_ge(S["n_ready"], layer * B + b + 1)
                    sp.dma_start(n_dram[b * T:(b + 1) * T, :].rearrange("(t p) d -> p t d", p=P),
                                 N[:, b * TT:(b + 1) * TT, :]).then_inc(S["n_stored"], 16)
                sp.wait_ge(S["owners_ready"], layer + 1)
                for i in range(DEEP):
                    load_weights(i, i)

                def reload(it, i):
                    load_weights(it * DEEP + (DEEP + i), i, it * DEEP + (2 + layer * TILES + i + 1))

                again, rest = divmod(TILES - DEEP, DEEP)
                with sp.Fori(0, again) as it:
                    for i in range(DEEP):
                        reload(it, i)
                for i in range(rest):
                    reload(again, i)
                for i in range(DEEP):
                    sp.wait_ge(S[f"y_stored{i}"], 16 * uses(i) * (layer + 1))
                for b in range(B):
                    sp.dma_start(Y[:, b * TT:(b + 1) * TT, :],
                                 y_dram[b * T:(b + 1) * T, :].rearrange("(t p) d -> p t d", p=P)).then_inc(S[f"y_loaded{b}"], 16)

            for b in range(B):
                sp.wait_ge(S["ffn_done"], B + b + 1)
                sp.dma_start(out[b * T:(b + 1) * T, :].rearrange("(t p) d -> p t d", p=P),
                             X[:, b * TT:(b + 1) * TT, :]).then_inc(S["x_stored"], 16)
            sp.wait_ge(S["x_stored"], 16 * B)

        @block.gpsimd
        def _(pool):
            step = Tally(S["pool_step"])
            link(pool, step, nc.gpsimd.memset(nhalf[:, :], -0.5))
            link(pool, step, nc.gpsimd.memset(zero[:, :, :], 0.0))
            nc.gpsimd.memset(Qs[0][:, :, :].bitcast(F32), 0.0).then_inc(S["q_clear"], 1)

            def inverse_deviations(layer, rows, b, shifted=False):
                t = slice(b * TT, (b + 1) * TT)
                n = stat_number(layer, rows, b)
                pool.wait_ge(S["stat_done"], n)
                if shifted:
                    step.add(nc.gpsimd.tensor_scalar(shift[:, t], mv[:, t, 0], -1.0, None, ALU.mult))
                link(pool, step, nc.gpsimd.tensor_scalar(rstd[:, t, 0], mv[:, t, 1], EPS, 1.0, ALU.add, ALU.mult))
                power = nc.gpsimd.tensor_tensor(rstd[:, t, 0], rstd[:, t, 0], nhalf[:, t], ALU.pow)
                if shifted:
                    link(pool, step, power)
                    power = nc.gpsimd.tensor_tensor(shift[:, t], shift[:, t], rstd[:, t, 0], ALU.mult)
                power.then_inc(S["rstd_ready"], 1)

            def last_part(layer, b):
                n = layer * B + b
                pool.wait_ge(S["mids_ready"], 2 * n + 2)
                nc.gpsimd.tensor_tensor(parts[:, b % 2, 1, 2, :], rest[:, b % 2, 1, :], parts[:, b % 2, 1, 1, :],
                                        ALU.subtract).then_inc(S["k_parts"], 1)

            def split_max(buf, ring_read):
                m, part = M[:, buf, :, :], Mp[:, buf, :, :, :]
                pool.wait_ge(S["ring_read"], ring_read)
                link(pool, step, nc.gpsimd.tensor_tensor(part[:, :, 0, :], m, zero[:, :, :], ALU.add))
                link(pool, step, nc.gpsimd.tensor_tensor(Mr[:, :, :], m, part[:, :, 0, :], ALU.subtract))
                link(pool, step, nc.gpsimd.tensor_tensor(part[:, :, 1, :], Mr[:, :, :], zero[:, :, :], ALU.add))
                nc.gpsimd.tensor_tensor(part[:, :, 2, :], Mr[:, :, :], part[:, :, 1, :], ALU.subtract).then_inc(S["max_split"], 1)

            def freed(layer, j):
                pool.wait_ge(S[f"y_stored{j % DEEP}"], filled_by(layer, 0, j))
                pool.sem_inc(S["yt_free"], 1)

            for layer in range(2):
                for rows, b in PREP_ORDER[layer]:
                    inverse_deviations(layer, rows, b, shifted=(rows == "u"))
                for b in range(B - 1):
                    last_part(layer, b)
                read0 = layer * (DPRO + 2 * DPER)
                split_max(0, read0 + 16)
                last_part(layer, B - 1)
                if layer == 0:
                    nc.gpsimd.memset(Qs[1][:, :, :].bitcast(F32), 0.0).then_inc(S["q_clear"], 1)
                with pool.Fori(0, 2) as it:
                    step.enter(it, 2 * GROUPS * 3)
                    for k in range(2 * GROUPS):
                        n_read = DVE_READ[("max",) + lookahead(k - 1, 7, 1)] if k else 0
                        split_max((k + 1) % 2, it * DPER + (read0 + DPRO + n_read))
                step.leave(2)
                for b in range(B):
                    inverse_deviations(layer, "ffn", b)
                pool.wait_ge(S["tiles_ready"], layer + 1)
                nc.gpsimd.tensor_tensor(inTile[:, :, 0, :], isTile[:, :, :], pr("back").unsqueeze(2).to_broadcast([P, NT, COLS]),
                                        ALU.mult).then_inc(S["pool_places"], 1)
                pool.wait_ge(S["tokens_ready"], layer + 1)
                pool.wait_ge(S["n_stored"], 16 * B * (layer + 1))

                def fetch(j):
                    nc.gpsimd.indirect_dma_start(xt[:, j % DEEP, :], None, n_dram,
                                                 bass.IndirectOffsetOnAxis(tok_in[:, j:j + 1], 0)).then_inc(S[f"xt_loaded{j % DEEP}"], 16)

                for j in range(DEEP):
                    fetch(j)
                for j in range(TILES):
                    if j + DEEP < TILES:
                        pool.wait_ge(S["xt_full"], layer * TILES + j + 1)
                        fetch(j + DEEP)
                    pool.wait_ge(S["y_ready"], 2 + layer * TILES + j + 1)
                    nc.gpsimd.indirect_dma_start(y_dram, bass.IndirectOffsetOnAxis(tok_out[:, j:j + 1], 0),
                                                 yt[:, j % DEEP, :], None).then_inc(S[f"y_stored{j % DEEP}"], 16)
                    if j >= BEHIND:
                        freed(layer, j - BEHIND)
                for j in range(TILES - BEHIND, TILES):
                    freed(layer, j)
                if layer == 0:
                    for b in range(B):
                        inverse_deviations(layer, "attn", b)

        @block.tensor
        def _(pe):
            ident = pr("ident")
            mm = nc.tensor.matmul
            pe.wait_ge(S["loaded"], 16)
            pe.wait_ge(S["setup_done"], 1)

            def stage_prep(layer):
                for b in range(B):
                    n = layer * B + b
                    pe.wait_ge(S["rows_ready"], n + 1)
                    for c in range(TT):
                        last = nc.tensor.transpose(PS[:, 2, c * P:(c + 1) * P], Nb[:, b % 2, c, :], ident)
                    last.then_inc(S["hT_filled"], 1)
                    pe.wait_ge(S["hT_ready"], n + 1)
                    if b:
                        pe.wait_ge(S["rests_ready"], 2 * n)
                    for j, w in enumerate(("wq", "wk")):
                        mm(PS[:, 3 + j, :], pr(w), hT[:, b % 2, :], start=True, stop=True).then_inc(S["qkv_filled"], 1)
                    if b:
                        pe.wait_ge(S["v_read"], n)
                    for c in range(TT):
                        last = mm(PS[:, 5, c * P:(c + 1) * P], hT[:, b % 2, c * P:(c + 1) * P], pr("wv"), start=True, stop=True)
                    last.then_inc(S["qkv_filled"], 1)
                    if layer == 0 and b == 0:
                        pe.wait_ge(S["gates_ready"], 1)
                        mm(PS[:, 7, 0:E], pr("ones"), gateW[:, :], start=True, stop=True)
                        mm(PS[:, 7, E:2 * E], xT[0][:, :], pr("gate_w"), start=True, stop=True).then_inc(S["gates_full"], 1)
                if layer == 0:
                    pe.wait_ge(S["gates_read"], 1)
                first_maxima(layer)
                second_maxima(layer)

            def max_scores(slot_, i, h, c):
                return mm(PS[:, slot_, :], Qs[i][0:SROWS, h, c * P:(c + 1) * P], Ks[i][0:SROWS, h // 2, :],
                          start=True, stop=True)

            def max_columns(slot_, buf):
                bank = PS[0:PARTS * GROUP, slot_, :].bitcast(BF16)
                for c in range(TT):
                    last = nc.tensor.transpose(bank[:, c * P:(c + 1) * P],
                                               Mp[:, buf, c, :, :].rearrange("p a j -> p (a j)"), identb[:, :])
                return last

            def first_maxima(layer):
                read0 = layer * (DPRO + 2 * DPER)
                pe.wait_ge(S["qk_loaded0"], layer * 3 * 16 * LDQK + 16 * LDQK)
                for e in range(16):
                    if e >= 3:
                        pe.wait_ge(S["ring_read"], read0 + e - 2)
                    max_scores(ring_bank(e), 0, e // TT, e % TT).then_inc(S["ring_full"], 1)

            def second_maxima(layer):
                read0, splits = layer * (DPRO + 2 * DPER), layer * (1 + 2 * 2 * GROUPS)
                pe.wait_ge(S["ring_read"], read0 + 14)
                pe.wait_ge(S["max_split"], splits + 1)
                max_columns(ring_bank(16), 0).then_inc(S["ring_full"], 1)
                for e in range(16):
                    if e == 2:
                        pe.wait_ge(S["maxT_ready"], splits + 1)
                    else:
                        pe.wait_ge(S["ring_read"], read0 + 15 + e if e < 2 else read0 + 14 + e)
                    max_scores(ring_bank(17 + e), 0, GROUP + e // TT, e % TT).then_inc(S["ring_full"], 1)

            def stage_heads(layer):
                start = layer * (PRO + 2 * PER)
                splits = layer * (1 + 2 * 2 * GROUPS)
                read0 = layer * (DPRO + 2 * DPER)
                if layer == 0:
                    pe.wait_ge(S["k_ones"], 32)
                pe.wait_ge(S["rests_ready"], 2 * B * (layer + 1))
                pe.wait_ge(S["v_read"], B * (layer + 1))
                with pe.Fori(0, 2) as it:
                    def fill(key):
                        r = RING[key]
                        before = ORDER[r - 3]
                        if r >= 3 and before[0] == "mT":
                            pe.wait_ge(S["maxT_ready"], it * (2 * GROUPS) + (splits + 1 + before[1]))
                        else:
                            n = DVE_READ[before] if r >= 3 else 0
                            pe.wait_ge(S["ring_read"], it * DPER + (read0 + DPRO + n))
                        return ring_bank(PRO + r)

                    def max_pass(k, h, c):
                        kk = k % (2 * GROUPS)
                        s = fill(("max", k, h, c))
                        max_scores(s, kk // GROUPS, (kk % GROUPS) * GROUP + h, c).then_inc(S["ring_full"], 1)

                    def values(k, kc):
                        i, half, y = k // GROUPS, kc // 2, kc % 2
                        w = it * (8 * 2 * GROUPS) + (layer * 32 * 2 * GROUPS // 2 + 8 * k + 4 * half + 4 + 2)
                        pe.wait_ge(S["exp_done"], w)
                        for j in range(GROUP):
                            h = (k % GROUPS) * GROUP + j
                            last = mm(PS[32 * j:32 * j + VW, 6, :], Vs[i][:, kc, h, :],
                                      Pb[:, 4 * half + j, y, :], start=(kc == 0), stop=(kc == TT - 1))
                        if y == 1:
                            last.then_inc(S["pv_done"], 1)

                    def head_rows(k):
                        s = fill(("oT", k))
                        pe.wait_ge(S["o_read"], it * (2 * GROUPS) + (layer * 4 * GROUPS + k + 1))
                        for c in range(TT):
                            last = nc.tensor.transpose(PS[:, s, c * P:(c + 1) * P], oS[:, k % 2, c * P:(c + 1) * P], ident)
                        last.then_inc(S["ring_full"], 1)

                    def outputs_T(i):
                        s = fill(("OT", i))
                        pe.wait_ge(S["ring_read"], it * DPER + (read0 + DPRO + DVE_READ["oT", GROUPS * (i + 1) - 1]))
                        for c in range(TT):
                            last = nc.tensor.transpose(PS[:, s, c * P:(c + 1) * P], O[:, c, :], ident)
                        last.then_inc(S["ring_full"], 1)

                    def project(i):
                        s = fill(("wo", i))
                        pe.wait_ge(S["ring_read"], it * DPER + (read0 + DPRO + DVE_READ["OT", i]))
                        for c in range(TT):
                            last = mm(PS[:, s, c * P:(c + 1) * P], OT[:, c * P:(c + 1) * P], pr("wo"), start=True, stop=True)
                        last.then_inc(S["ring_full"], 1)

                    for k in range(2 * GROUPS):
                        i = k // GROUPS
                        if k % GROUPS == 0:
                            pe.wait_ge(S[f"v_loaded{i}"], it * 16 + (layer * (3 - i) * 16 + 16))
                        pe.wait_ge(S["max_loaded"], it * (16 * PARTS * 2 * GROUPS) + 16 * PARTS * (splits + 1 + k))
                        for u in range(8):
                            j, half = u % 4, u // 4
                            h = (k % GROUPS) * GROUP + j
                            pe.wait_ge(S["exp_done"], it * (16 * GROUPS) + (layer * 32 * GROUPS + 8 * k + u + 1))
                            for y in range(2):
                                kc = 2 * half + y
                                last = mm(PS[:, 2 + 2 * (u % 2) + y, :], Ks[i][0:SROWS + PARTS, h // 2, kc * P:(kc + 1) * P],
                                          Qs[i][0:SROWS + PARTS, h, :], start=True, stop=True)
                            last.then_inc(S["scores_full"], 1)
                            if not at_end(k, u):
                                if u == 0 and (k + 2) % GROUPS == 0:
                                    nxt = (k + 2) // GROUPS % 2
                                    pe.wait_ge(S[f"qk_loaded{nxt}"],
                                               it * (16 * LDQK) + 16 * LDQK * (layer * (3 - nxt) + 1 + (1 - nxt)))
                                for y in range(2):
                                    max_pass(*lookahead(k, u, y))
                            if u in (0, 2) and k:
                                values(k - 1, 2 + u // 2)
                            if u == 3:
                                s = fill(("mT", k + 1))
                                pe.wait_ge(S["max_split"], it * (2 * GROUPS) + (splits + 2 + k))
                                max_columns(s, (k + 1) % 2).then_inc(S["ring_full"], 1)
                            if u == 4 and k:
                                head_rows(k - 1)
                            if u in (5, 7):
                                values(k, u // 7)
                            if u == 7 and k == GROUPS:
                                outputs_T(0)
                            if u == 0 and k == GROUPS + 1:
                                project(0)
                    late = [lookahead(k, u, y) for u in LATE for y in range(2)]
                    chunks = [2, 3]
                    for what in TAIL:
                        if what == "values":
                            values(k, chunks.pop(0))
                        elif what == "max":
                            max_pass(*late.pop(0))
                        elif what == "oT":
                            head_rows(k)
                        elif what == "OT":
                            outputs_T(1)
                        else:
                            project(1)

            def logits(layer, b):
                pe.wait_ge(S["hT2_ready"], layer * B + b + 1)
                for c in range(TT):
                    t = b * TT + c
                    last = mm(PS[:, 4, t * E:(t + 1) * E], hT2[:, b, c * P:(c + 1) * P], gateW[:, :], start=True, stop=True)
                last.then_inc(S["logits_full"], 1)

            def stage_routing(layer):
                pe.wait_ge(S["u_ready"], layer + 1)
                for b in range(B):
                    for c in range(TT):
                        last = nc.tensor.transpose(PS[:, b, c * P:(c + 1) * P], U[:, b * TT + c, :], ident)
                    last.then_inc(S["hT2_filled"], 1)
                    if b:
                        logits(layer, b - 1)
                logits(layer, B - 1)
                pe.wait_ge(S["hot_ready"], layer + 1)
                full = PS[:, 7, 0:(NT + 1) * E]
                mm(full, allb[:, :], hot[:, NT:NT + 1, :].to_broadcast([P, NT + 1, E]), start=True, stop=False)
                for t in range(NT):
                    mm(PS[:, 7, (t + 1) * E:(NT + 1) * E], allb[:, :], hot[:, t:t + 1, :].to_broadcast([P, NT - t, E]),
                       start=False, stop=False)
                mm(full, beforeb[:, :], hot[:, :, :].rearrange("p t e -> p (t e)"), start=False, stop=True).then_inc(S["ranks_full"], 1)
                for b in range(B):
                    pe.wait_ge(S["places_ready"], layer * B + b + 1)
                    if b == 0:
                        pe.wait_ge(S["pool_places"], layer + 1)
                    for t in range(b * TT, (b + 1) * TT):
                        last = mm(PS[:, 6, 0:2 * COLS], atPlace[:, t, :], inTile[:, t, :, :].rearrange("p a j -> p (a j)"),
                                  start=(t == 0), stop=(t == NT - 1))
                last.then_inc(S["tokens_full"], 1)

            def stage_experts(layer):
                done = layer * TILES

                def turn(it, i):
                    pe.wait_ge(S[f"xt_loaded{i % DEEP}"], filled_by(layer, it, i))
                    nc.tensor.transpose(PS[:, i % 2, 0:P], xt[:, i % DEEP, :], ident).then_inc(S["xt_full"], 1)

                def hidden(it, i):
                    pe.wait_ge(S[f"w_loaded{i % DEEP}"], filled_by(layer, it, i))
                    pe.wait_ge(S["xT_ready"], it * DEEP + (done + i + 1))
                    for c in range(FC):
                        last = mm(PS[:, 2 + i % 2, c * P:(c + 1) * P], W[i % DEEP][:, c * P:(c + 1) * P], xT[i % 2][:, :],
                                  start=True, stop=True)
                    last.then_inc(S["mid_full"], 1)

                def result(it, i):
                    pe.wait_ge(S["y_ready"], it * DEEP + (done + i + 1))
                    pe.wait_ge(S["mid_ready"], it * DEEP + (done + i + 1))
                    for c in range(FC):
                        last = mm(PS[:, 4 + i % 2, 0:P], mid[i % 2][:, c, :], W[i % DEEP][:, F + c * P:F + (c + 1) * P],
                                  start=(c == 0), stop=(c == FC - 1))
                    last.then_inc(S["y_full"], 1)

                turn(0, 0)
                turn(0, 1)
                hidden(0, 0)
                with pe.Fori(0, LOOPS) as it:
                    for i in range(1, DEEP + 1):
                        turn(it, i + 1)
                        hidden(it, i)
                        result(it, i - 1)
                for i in range(1, REST + 1):
                    if i < REST:
                        turn(LOOPS, i + 1)
                    hidden(LOOPS, i)
                    result(LOOPS, i - 1)
                result(LOOPS, REST)

            def stage_attention():
                def front(b, c):
                    hb = hT[:, b % 2, :]
                    if c == 0:
                        pe.wait_ge(S["a_rows"], b + 1)
                        if b:
                            pe.wait_ge(S["a_qk_read"], 2 * b)
                        for t in range(TT):
                            last = nc.tensor.transpose(PS[:, 0, t * P:(t + 1) * P], Nb[:, b % 2, t, :], ident)
                        last.then_inc(S["a_hT_filled"], 1)
                    elif c == 1:
                        pe.wait_ge(S["a_hT_ready"], b + 1)
                        if b:
                            pe.wait_ge(S["a_v_read"], b)
                        mm(PS[:, 1, :], pr("aq"), hb, start=True, stop=True).then_inc(S["a_qkv_full"], 1)
                    elif c == 2:
                        mm(PS[:, 0, :], pr("ak"), hb, start=True, stop=True).then_inc(S["a_qkv_full"], 1)
                    else:
                        pe.wait_ge(S["a_qk_read"], 2 * b + 1)
                        for t in range(TT):
                            last = mm(PS[:, 1, t * P:(t + 1) * P], hb[:, t * P:(t + 1) * P], pr("av"), start=True, stop=True)
                        last.then_inc(S["a_qkv_full"], 1)

                def scores(b, c):
                    w, n = (c + 1) * P, b * TT + c
                    if c == 0:
                        pe.wait_ge(S["a_qk_read"], 2 * (b + 1))
                    if n >= 2:
                        pe.wait_ge(S["a_exp"], n - 1)
                    mm(PS[:, 3 + c % 2, 0:w], AT_q[b % 2][:, c * P:w], AT_k[b % 2][:, 0:w],
                       start=True, stop=True).then_inc(S["a_s_full"], 1)

                def turned_read(b, c):
                    if c == TT - 1:
                        pe.wait_ge(S["a_pT3_read"], b + 1)
                    else:
                        pe.wait_ge(S["a_pT_read"], (TT - 1) * b + c + 1)

                def turn(b, c):
                    pe.wait_ge(S["a_exp"], b * TT + c + 1)
                    if b * TT + c >= 2:
                        turned_read((b * TT + c - 2) // TT, (c - 2) % TT)
                    for kc in range(c + 1):
                        last = nc.tensor.transpose(PS[:, 5 + c % 2, kc * P:(kc + 1) * P], AT_p[b % 2][:, c, kc * P:(kc + 1) * P], ident)
                    last.then_inc(S["a_pT_full"], 1)

                def sums(b, c):
                    turned_read(b, c)
                    if c == 0:
                        pe.wait_ge(S["a_v_read"], b + 1)
                        if b >= 2:
                            pe.wait_ge(S["a_o_read"], b - 1)
                    for kc in range(c + 1):
                        last = mm(PS[:, SUMS[b % 2], c * P:(c + 1) * P], AT_pT[c % 2][:, kc * P:(kc + 1) * P],
                                  AT_v[b][:, kc * P:(kc + 1) * P], start=(kc == 0), stop=(kc == c))
                    if c == TT - 1:
                        last.then_inc(S["a_o_full"], 1)

                for c in range(TT):
                    front(0, c)
                for s in range(B + 1):
                    for c in range(TT):
                        if s < B:
                            scores(s, c)
                        if s:
                            turn(s - 1, c)
                        if s < B - 1:
                            front(s + 1, c)
                        if s and c:
                            sums(s - 1, c - 1)
                        elif s >= 2:
                            sums(s - 2, TT - 1)
                sums(B - 1, TT - 1)

            for layer in range(2):
                stage_prep(layer)
                stage_heads(layer)
                stage_routing(layer)
                stage_experts(layer)
                if layer == 0:
                    stage_attention()

        @block.scalar
        def _(act):
            activation = nc.scalar.activation
            act.wait_ge(S["loaded"], 16)
            activation(amx[:, 0, 0:1], pr("row"), ACT.Exp, scale=-1.0)
            act.wait_ge(S["setup_done"], 1)

            def stage_prep(layer):
                def rows(b):
                    act.wait_ge(S["rstd_ready"], stat_number(layer, "u", b))
                    if b >= 2:
                        act.wait_ge(S["hT_filled"], layer * B + b - 1)
                    for c in range(TT):
                        t = b * TT + c
                        last = activation(Nb[:, b % 2, c, :], U[:, t, :], ACT.Identity, bias=shift[:, t:t + 1], scale=rstd[:, t, :])
                    last.then_inc(S["rows_ready"], 1)

                def turned(b):
                    act.wait_ge(S["hT_filled"], layer * B + b + 1)
                    activation(hT[:, b % 2, :], PS[:, 2, :], ACT.Identity, bias=pr("b1"), scale=pr("g1")).then_inc(S["hT_ready"], 1)

                def firsts(b):
                    n = layer * B + b
                    if n >= 2:
                        act.wait_ge(S[f"parts_stored{b % 2}"], n // 2 * STORED)
                    for j, bias in ((0, "bq"), (1, "bk")):
                        act.wait_ge(S["qkv_filled"], 3 * n + 1 + j)
                        activation(parts[:, b % 2, j, 0, :], PS[:, 3 + j, :], ACT.Identity, bias=pr(bias)).then_inc(S["firsts_ready"], 1)

                def mids(b):
                    for j in range(2):
                        act.wait_ge(S["rests_ready"], 2 * (layer * B + b) + j + 1)
                        activation(parts[:, b % 2, j, 1, :], rest[:, b % 2, j, :], ACT.Copy).then_inc(S["mids_ready"], 1)

                rows(0)
                turned(0)
                rows(1)
                firsts(0)
                for b in range(1, B):
                    turned(b)
                    mids(b - 1)
                    if b < B - 1:
                        rows(b + 1)
                    firsts(b)
                mids(B - 1)

            def stage_heads(layer):
                start = layer * (PRO + 2 * PER)
                act.wait_ge(S["ring_full"], start + 17)
                activation(MT[:, 0, :], PS[0:PARTS * GROUP, ring_bank(16), :].bitcast(BF16)[:, 0:T], ACT.Copy).then_inc(S["maxT_ready"], 1)
                with act.Fori(0, 2) as it:
                    def filled(key):
                        act.wait_ge(S["ring_full"], it * PER + (start + PRO + RING[key] + 1))
                        return ring_bank(PRO + RING[key])

                    def read_heads(k):
                        act.wait_ge(S["pv_done"], it * (4 * GROUPS) + (layer * 8 * GROUPS + 2 * k + 2 + 2))
                        activation(oS[:, k % 2, :], PS[:, 6, :], ACT.Copy).then_inc(S["o_read"], 1)

                    for k in range(2 * GROUPS):
                        for u in range(8):
                            half = u // 4
                            act.wait_ge(S["scores_full"], it * (16 * GROUPS) + (layer * 32 * GROUPS + 8 * k + u + 1))
                            if u % 4 == 0:
                                act.wait_ge(S["pv_done"], it * (4 * GROUPS) + (layer * 8 * GROUPS + 2 * k + half + 1))
                            activation(Pb[:, u, :, :], PS[:, 2 + 2 * (u % 2):4 + 2 * (u % 2), :], ACT.Exp,
                                       scale=float(HD) ** -0.5).then_inc(S["exp_done"], 1)
                            if u == 2 and k:
                                read_heads(k - 1)
                            if u == 3:
                                s = filled(("mT", k + 1))
                                activation(MT[:, (k + 1) % 2, :], PS[0:PARTS * GROUP, s, :].bitcast(BF16)[:, 0:T],
                                           ACT.Copy).then_inc(S["maxT_ready"], 1)
                    read_heads(2 * GROUPS - 1)

            def stage_routing(layer):
                for b in range(B):
                    act.wait_ge(S["hT2_filled"], layer * B + b + 1)
                    activation(hT2[:, b, :], PS[:, b, :], ACT.Copy).then_inc(S["hT2_ready"], 1)

            def stage_experts(layer):
                def rectify(it, i):
                    act.wait_ge(S["mid_full"], it * DEEP + (layer * TILES + i + 1))
                    for c in range(FC):
                        last = activation(mid[i % 2][:, c, :], PS[:, 2 + i % 2, c * P:(c + 1) * P], ACT.Relu,
                                          bias=W[i % DEEP][:, 2 * F + c:2 * F + c + 1])
                    last.then_inc(S["mid_ready"], 1)

                rectify(0, 0)
                with act.Fori(0, LOOPS) as it:
                    for i in range(1, DEEP + 1):
                        rectify(it, i)
                for i in range(1, REST + 1):
                    rectify(LOOPS, i)

            def stage_attention():
                def front(b, c):
                    if c == 0:
                        act.wait_ge(S["a_hT_filled"], b + 1)
                        activation(hT[:, b % 2, :], PS[:, 0, :], ACT.Copy).then_inc(S["a_hT_ready"], 1)
                        return
                    act.wait_ge(S["a_qkv_full"], b * 3 + c)
                    if c == 1:
                        activation(AT_q[b % 2], PS[:, 1, :], ACT.Copy, scale=float(P) ** -0.5).then_inc(S["a_qk_read"], 1)
                    elif c == 2:
                        activation(AT_k[b % 2], PS[:, 0, :], ACT.Copy).then_inc(S["a_qk_read"], 1)
                    else:
                        activation(AT_v[b], PS[:, 1, :], ACT.Copy).then_inc(S["a_v_read"], 1)

                for c in range(TT):
                    front(0, c)
                for s in range(B + 1):
                    for c in range(TT):
                        if s < B:
                            w = (c + 1) * P
                            act.wait_ge(S["a_max"], s * TT + c + 1)
                            activation(AT_p[s % 2][:, c, 0:w], PS[:, 3 + c % 2, 0:w], ACT.Exp, bias=amx[:, s % 2, c:c + 1],
                                       accum_out=asum[:, s, c:c + 1]).then_inc(S["a_exp"], 1)
                        if s and c == TT - 1:
                            act.wait_ge(S["a_pT_full"], (s - 1) * TT + c + 1)
                            activation(AT_pT[c % 2], PS[:, 5 + c % 2, :], ACT.Copy).then_inc(S["a_pT3_read"], 1)
                        if s < B - 1:
                            front(s + 1, c)

            for layer in range(2):
                stage_prep(layer)
                stage_heads(layer)
                stage_routing(layer)
                stage_experts(layer)
                if layer == 0:
                    stage_attention()

        @block.vector
        def _(dve):
            v = nc.vector
            step = Tally(S["dve_step"])
            v.memset(PS[:, 6, :], 0.0)
            v.memset(onesb[:, :], 1.0).then_inc(S["ones_ready"], 1)
            v.memset(Vall[:, :, :].rearrange("p b (c w) -> p (b c) w", w=VW)[:, :, HD:VW], 1.0).then_inc(S["v_ones"], 1)

            def setup():
                dve.wait_ge(S["loaded"], 16)
                link(dve, step, v.tensor_copy(identb[:, :], pr("ident")))
                v.tensor_scalar(gateW[:, :], pr("gate_w"), pr("g2"), None, ALU.mult)
                link(dve, step, v.tensor_scalar(xT[0][:, :], pr("ones"), pr("b2"), None, ALU.mult))
                dve.sem_inc(S["gates_ready"], 1)
                v.tensor_copy(beforeb[:, :], pr("before"))
                v.memset(allb[:, :], 1.0)
                link(dve, step, v.memset(hot[:, NT, :], 0.0))
                for name, n in (("pv_done", 2), ("exp_done", 2), ("y_ready", 2),
                                ("yt_free", DEEP), ("setup_done", 1)):
                    dve.sem_inc(S[name], n)

            def statistics(layer, rows, b, src):
                for t in range(b * TT, (b + 1) * TT):
                    step.add(v.bn_stats(stats[:, t, :], src[:, t, :]))
                dve.wait_ge(step.sem, step.now())
                for t in range(b * TT, (b + 1) * TT):
                    last = v.bn_aggr(mv[:, t, :], stats[:, t, :])
                last.then_inc(S["stat_done"], 1)

            def normalise(layer, rows, b, dst, src):
                dve.wait_ge(S["rstd_ready"], stat_number(layer, rows, b))
                for c in range(TT):
                    t = b * TT + c
                    last = v.tensor_scalar(dst[:, c, :], src[:, t, :], mv[:, t, 0:1], rstd[:, t, :], ALU.subtract, ALU.mult)
                return last

            def prep_statistics(layer, i):
                rows, b = PREP_ORDER[layer][i]
                if rows == "x":
                    if layer == 0:
                        dve.wait_ge(S[f"x_loaded{b}"], 16)
                    statistics(layer, "x", b, X)
                else:
                    link(dve, step, normalise(layer, "x", b, U[:, b * TT:(b + 1) * TT, :], X))
                    statistics(layer, "u", b, U)

            def stage_prep(layer):
                def rests(b):
                    n = layer * B + b
                    for j, bias in ((0, "bq"), (1, "bk")):
                        dve.wait_ge(S["firsts_ready"], 2 * n + j + 1)
                        v.scalar_tensor_tensor(rest[:, b % 2, j, :], PS[:, 3 + j, :], pr(bias), parts[:, b % 2, j, 0, :],
                                               ALU.add, ALU.subtract).then_inc(S["rests_ready"], 1)
                    dve.wait_ge(S["qkv_filled"], 3 * n + 3)
                    Vb = Vall[:, b, :].rearrange("p (c h w) -> p c h w", h=NH, w=VW)
                    v.tensor_tensor(Vb[:, :, :, 0:HD], PS[:, 5, :].rearrange("p (c h d) -> p c h d", c=TT, d=HD),
                                    pr("bv").rearrange("p (h d) -> p h d", d=HD).unsqueeze(1).to_broadcast([P, TT, NH, HD]),
                                    ALU.add).then_inc(S["v_read"], 1)

                def thirds(b):
                    n = layer * B + b
                    dve.wait_ge(S["mids_ready"], 2 * n + 1)
                    v.tensor_tensor(parts[:, b % 2, 0, 2, :], rest[:, b % 2, 0, :], parts[:, b % 2, 0, 1, :],
                                    ALU.subtract).then_inc(S["q_parts"], 1)

                for i in range(2 * B):
                    if layer == 0 or i >= PREPARED:
                        prep_statistics(layer, i)
                    if layer == 0 and i == 3:
                        setup()
                if layer == 0:
                    dve.wait_ge(S["v_ones"], 1)
                for b in range(B):
                    if b == B - 1:
                        first_maxima(layer)
                    rests(b)
                    thirds(b)
                    if layer == 0 and b == 1:
                        dve.wait_ge(S["gates_full"], 1)
                        v.tensor_copy(gateC[:, 0, :], PS[:, 7, 0:E])
                        v.tensor_tensor(gateB[:, 0, :], PS[:, 7, E:2 * E], pr("gate_b"), ALU.add).then_inc(S["gates_read"], 1)
                second_maxima(layer)

            def row_max(slot_, buf, h, c):
                v.tensor_reduce(M[:, buf, c, h:h + 1], PS[:, slot_, :], AX.X, ALU.max, negate=True).then_inc(S["ring_read"], 1)

            def first_maxima(layer):
                for e in range(16):
                    dve.wait_ge(S["ring_full"], layer * (PRO + 2 * PER) + e + 1)
                    row_max(ring_bank(e), 0, e // TT, e % TT)

            def second_maxima(layer):
                for e in range(16):
                    dve.wait_ge(S["ring_full"], layer * (PRO + 2 * PER) + 17 + e + 1)
                    row_max(ring_bank(17 + e), 1, e // TT, e % TT)

            def stage_heads(layer):
                start = layer * (PRO + 2 * PER)
                read0 = layer * (DPRO + 2 * DPER)

                with dve.Fori(0, 2) as it:
                    step.enter(it, 2 * GROUPS + 2)

                    def filled(key):
                        dve.wait_ge(S["ring_full"], it * PER + (start + PRO + RING[key] + 1))
                        return ring_bank(PRO + RING[key])

                    def max_pass(k, h, c):
                        row_max(filled(("max", k, h, c)), k % 2, h, c)

                    def normalise_heads(k):
                        s = filled(("oT", k))
                        bank = PS[:, s, :].rearrange("p (c j w) -> p c j w", c=TT, j=GROUP)
                        link(dve, step, v.reciprocal(rden[:, :, :, :], bank[:, :, :, HD:HD + 1]))
                        h0 = (k % GROUPS) * GROUP * HD
                        v.tensor_tensor(O[:, :, h0:h0 + GROUP * HD].rearrange("p c (j d) -> p c j d", d=HD),
                                        bank[:, :, :, 0:HD], rden[:, :, :, :].to_broadcast([P, TT, GROUP, HD]),
                                        ALU.mult).then_inc(S["ring_read"], 1)

                    def outputs_T(i):
                        s = filled(("OT", i))
                        v.tensor_copy(OT[:, :], PS[:, s, :]).then_inc(S["ring_read"], 1)

                    def project(i):
                        s = filled(("wo", i))
                        Ub = U[:, bass.ds((it * 2 + i) * TT, TT), :]
                        bo = pr("bo").unsqueeze(1).to_broadcast([P, TT, P])
                        v.tensor_tensor(tmp[:, :, :], PS[:, s, :].rearrange("p (c d) -> p c d", d=P), bo, ALU.add)\
                            .then_inc(S["ring_read"], 1)
                        dve.wait_ge(S["ring_read"], it * DPER + (read0 + DPRO + DVE_READ["wo", i]))
                        link(dve, step, v.tensor_tensor(Ub, Ub, tmp[:, :, :], ALU.add))

                    for k in range(2 * GROUPS):
                        for u in range(8):
                            if not at_end(k, u):
                                for y in range(2):
                                    max_pass(*lookahead(k, u, y))
                            if u == 4 and k:
                                normalise_heads(k - 1)
                            if u == 7 and k == GROUPS:
                                outputs_T(0)
                            if u == 0 and k == GROUPS + 1:
                                project(0)
                    late = [lookahead(k, u, y) for u in LATE for y in range(2)]
                    for what in TAIL:
                        if what == "max":
                            max_pass(*late.pop(0))
                        elif what == "oT":
                            normalise_heads(k)
                        elif what == "OT":
                            outputs_T(1)
                        elif what == "wo":
                            project(1)
                step.leave(2)

            def stage_routing(layer):
                dve.wait_ge(S["ring_read"], (layer + 1) * (DPRO + 2 * DPER))
                dve.sem_inc(S["u_ready"], 1)
                for b in range(B):
                    statistics(layer, "ffn", b, U)

                def rows(b):
                    normalise(layer, "ffn", b, N[:, b * TT:(b + 1) * TT, :], U).then_inc(S["n_ready"], 1)

                rows(0)
                each = [P, NT, E]
                io = pr("iota").unsqueeze(1).to_broadcast(each)
                dve.wait_ge(S["stat_done"], stat_number(layer, "ffn", B - 1))
                link(dve, step, v.tensor_tensor(L2[:, :, :], mv[:, :, 0:1].to_broadcast(each), gateC[:, :, :].to_broadcast(each), ALU.mult))
                rows(1)
                dve.wait_ge(S["logits_full"], B * (layer + 1))
                dve.wait_ge(S["rstd_ready"], stat_number(layer, "ffn", B - 1))
                link(dve, step, v.tensor_tensor(L[:, :, :], PS[:, 4, 0:NT * E].rearrange("p (t e) -> p t e", e=E), L2[:, :, :], ALU.subtract))
                link(dve, step, v.tensor_tensor(L[:, :, :], L[:, :, :], rstd[:, :, :].to_broadcast(each), ALU.mult))
                link(dve, step, v.tensor_tensor(L[:, :, :], L[:, :, :], gateB[:, :, :].to_broadcast(each), ALU.add))
                link(dve, step, v.tensor_reduce(mx[:, :, 0], L[:, :, :], AX.X, ALU.max))
                link(dve, step, v.tensor_tensor(L2[:, :, :], L[:, :, :], mx[:, :, :].to_broadcast(each), ALU.is_equal))
                link(dve, step, v.tensor_tensor(L[:, :, :], L2[:, :, :], io, ALU.mult))
                link(dve, step, v.tensor_reduce(mx[:, :, 0], L[:, :, :], AX.X, ALU.min))
                v.tensor_tensor(hot[:, 0:NT, :], io, mx[:, :, :].to_broadcast(each), ALU.is_equal).then_inc(S["hot_ready"], 1)
                for b in range(2, B):
                    rows(b)
                dve.wait_ge(S["ranks_full"], layer + 1)
                rank = PS[:, 7, 0:NT * E].rearrange("p (t e) -> p t e", e=E)
                link(dve, step, v.tensor_scalar(nti[:, :], PS[:, 7, NT * E:(NT + 1) * E], 1.0 / P, (P - 1.0) / P - 0.498, ALU.mult, ALU.add))
                link(dve, step, v.tensor_copy(nt[:, :], nti[:, :]))
                link(dve, step, v.tensor_tensor(lowers[:, :, :], nt[:, :].unsqueeze(1).to_broadcast([P, E, E]),
                                                pr("first").rearrange("p (a b) -> p a b", b=E), ALU.mult))
                link(dve, step, v.tensor_reduce(first[:, :], lowers[:, :, :], AX.X, ALU.add))
                link(dve, step, v.tensor_tensor(src[:, :, :], rank, first[:, :].unsqueeze(1).to_broadcast(each), ALU.add))
                link(dve, step, v.tensor_tensor(src[:, :, :], src[:, :, :], hot[:, 0:NT, :], ALU.mult))
                link(dve, step, v.tensor_reduce(slotf[:, :], src[:, :, :], AX.X, ALU.add))
                link(dve, step, v.tensor_scalar(tilei[:, :], slotf[:, :], 1.0 / P, -0.498, ALU.mult, ALU.add))
                link(dve, step, v.tensor_copy(tilef[:, :, 0], tilei[:, :]))
                step.add(v.scalar_tensor_tensor(placef[:, :, 0], tilef[:, :, 0], -float(P), slotf[:, :], ALU.mult, ALU.add))
                link(dve, step, v.tensor_tensor(isTile[:, :, :], pr("tile").unsqueeze(1).to_broadcast([P, NT, COLS]),
                                                tilef[:, :, :].to_broadcast([P, NT, COLS]), ALU.is_equal))
                dve.sem_inc(S["tiles_ready"], 1)
                v.tensor_scalar(inTile[:, :, 1, :], isTile[:, :, :], pr("row"), None, ALU.mult)
                for b in range(B):
                    t = slice(b * TT, (b + 1) * TT)
                    v.tensor_tensor(atPlace[:, t, :], pr("place").unsqueeze(1).to_broadcast([P, TT, P]),
                                    placef[:, t, :].to_broadcast([P, TT, P]), ALU.is_equal).then_inc(S["places_ready"], 1)
                link(dve, step, v.scalar_tensor_tensor(nt[:, :], first[:, :], 1.0 / P, nt[:, :], ALU.mult, ALU.add))
                link(dve, step, v.tensor_tensor(owner[:, :, :], pr("tile").unsqueeze(2).to_broadcast([P, COLS, E]),
                                                nt[:, :].unsqueeze(1).to_broadcast([P, COLS, E]), ALU.is_ge))
                link(dve, step, v.tensor_reduce(ownf[:, :], owner[:, :, :], AX.X, ALU.add))
                v.tensor_scalar(owni[:, :], ownf[:, :], float(E - 1), None, ALU.min).then_inc(S["owners_ready"], 1)
                dve.wait_ge(S["tokens_full"], layer + 1)
                dve.wait_ge(S["owners_ready"], layer + 1)
                link(dve, step, v.tensor_scalar(toks[:, :], PS[:, 6, 0:COLS], float(P), float(NT * P), ALU.mult, ALU.add))
                link(dve, step, v.tensor_tensor(toks[:, :], toks[:, :], PS[:, 6, COLS:2 * COLS], ALU.add))
                step.add(v.tensor_scalar(tok_in[:, :], toks[:, :], float(NT * P - 1), None, ALU.min))
                link(dve, step, v.scalar_tensor_tensor(ownf[:, :], toks[:, :], float(NT * P), pr("slot"), ALU.is_equal, ALU.mult))
                v.tensor_tensor(tok_out[:, :], toks[:, :], ownf[:, :], ALU.add).then_inc(S["tokens_ready"], 1)

            def stage_experts(layer):
                done = layer * TILES
                for b in range(B):
                    t = slice(b * TT, (b + 1) * TT)
                    add_half(X[:, t, :], U[:, t, :])

                def turned(it, i):
                    dve.wait_ge(S["xt_full"], it * DEEP + (done + i + 1))
                    v.tensor_scalar(xT[i % 2][:, :], PS[:, i % 2, 0:P], pr("g2"), pr("b2"), ALU.mult, ALU.add).then_inc(S["xT_ready"], 1)

                def result(it, i):
                    dve.wait_ge(S["yt_free"], it * DEEP + (done + i + 1))
                    dve.wait_ge(S["y_full"], it * DEEP + (done + i + 1))
                    v.tensor_tensor(yt[:, i % DEEP, :], PS[:, 4 + i % 2, 0:P], W[i % DEEP][:, 2 * F + FC:EW], ALU.add)\
                        .then_inc(S["y_ready"], 1)

                turned(0, 0)
                turned(0, 1)
                with dve.Fori(0, LOOPS) as it:
                    for i in range(1, DEEP + 1):
                        turned(it, i + 1)
                        result(it, i - 1)
                for i in range(1, REST + 1):
                    if i < REST:
                        turned(LOOPS, i + 1)
                    result(LOOPS, i - 1)
                result(LOOPS, REST)

            def add_half(dst, src):
                return v.scalar_tensor_tensor(dst.rearrange("p t d -> p (t d)"), src.rearrange("p t d -> p (t d)"), 0.5,
                                              dst.rearrange("p t d -> p (t d)"), ALU.mult, ALU.add)

            def finish_ffn(layer, b):
                dve.wait_ge(S[f"y_loaded{b}"], 16 * (layer + 1))
                t = slice(b * TT, (b + 1) * TT)
                add_half(X[:, t, :], Y[:, t, :]).then_inc(S["ffn_done"], 1)

            def stage_attention():
                def updated(b):
                    finish_ffn(0, b)
                    dve.wait_ge(S["ffn_done"], b + 1)
                    statistics(0, "attn", b, X)

                def rows(b):
                    if b >= 2:
                        dve.wait_ge(S["a_hT_filled"], b - 1)
                    normalise(0, "attn", b, Nb[:, b % 2, :, :], X).then_inc(S["a_rows"], 1)

                def maxima(b, c):
                    w = (c + 1) * P
                    dve.wait_ge(S["a_s_full"], b * TT + c + 1)
                    bank = PS[:, 3 + c % 2, :]
                    link(dve, step, v.tensor_tensor(bank[:, w - P:w], bank[:, w - P:w], pr("causal"), ALU.add))
                    v.tensor_reduce(amx[:, b % 2, c:c + 1], bank[:, 0:w], AX.X, ALU.max, negate=True).then_inc(S["a_max"], 1)

                def turned(b, c):
                    w = (c + 1) * P
                    dve.wait_ge(S["a_pT_full"], b * TT + c + 1)
                    v.tensor_copy(AT_pT[c % 2][:, 0:w], PS[:, 5 + c % 2, 0:w]).then_inc(S["a_pT_read"], 1)

                def add_up(b):
                    dve.wait_ge(S["a_o_full"], b + 1)
                    t = slice(b * TT, (b + 1) * TT)
                    link(dve, step, v.reciprocal(arec[:, :, 0], asum[:, b, :]))
                    v.tensor_tensor(tmp[:, :, :], PS[:, SUMS[b % 2], :].rearrange("p (c d) -> p c d", d=P),
                                    arec[:, :, :].to_broadcast([P, TT, P]), ALU.mult).then_inc(S["a_o_read"], 1)
                    dve.wait_ge(S["a_o_read"], b + 1)
                    link(dve, step, v.tensor_tensor(X[:, t, :], X[:, t, :], tmp[:, :, :], ALU.add))

                updated(0)
                updated(1)
                rows(0)
                updated(2)
                rows(1)
                updated(3)
                for s in range(B + 1):
                    for c in range(TT):
                        if s < B:
                            maxima(s, c)
                        if s and c < TT - 1:
                            turned(s - 1, c)
                        if c == 1 and s >= 2:
                            add_up(s - 2)
                        if (s, c) in NEXT:
                            prep_statistics(1, NEXT[s, c])
                    if s < 2:
                        rows(s + 2)
                add_up(B - 1)

            for layer in range(2):
                stage_prep(layer)
                stage_heads(layer)
                stage_routing(layer)
                stage_experts(layer)
                if layer == 0:
                    stage_attention()
            for b in range(B):
                finish_ffn(1, b)


def kernel(**inputs):
    import concourse.bacc as bacc
    from concourse.bass_utils import run_bass_kernel_spmd as run

    a = {k.removeprefix("L0_"): np.asarray(v) for k, v in inputs.items()}
    cols = {n: np.zeros((P, hi - lo), np.float32) for n, (lo, hi) in _AT.items()}
    for n in ("wq", "wk", "wv", "wo", "gate_w"):
        cols[n] = a["ffn_" + n]
    for n, m in (("aq", "attn_Wq"), ("ak", "attn_Wk"), ("av", "attn_Wv")):
        cols[n] = a[m]
    for n in ("bv", "bo", "gate_b"):
        cols[n] = np.broadcast_to(a["ffn_" + n][None, :], cols[n].shape)
    for n, m in (("g1", "ln1_g"), ("b1", "ln1_b"), ("g2", "ln2_g"), ("b2", "ln2_b"), ("bq", "bq"), ("bk", "bk")):
        cols[n] = a["ffn_" + m][:, None]
    i, j = np.arange(P)[:, None], np.arange(P)[None, :]
    cols["ident"] = (i == j).astype(np.float32)
    cols["before"] = (i < j).astype(np.float32)
    cols["ones"] = np.ones((P, P), np.float32)
    cols["causal"] = np.where(j <= i, 0.0, -3e38).astype(np.float32)
    cols["iota"] = np.broadcast_to(np.arange(E, dtype=np.float32)[None, :] - E, (P, E))
    cols["tile"] = np.broadcast_to(np.arange(COLS, dtype=np.float32)[None, :], (P, COLS))
    cols["place"] = np.broadcast_to(np.arange(P, dtype=np.float32)[None, :], (P, P))
    cols["slot"] = (np.arange(COLS)[None, :] * P + i).astype(np.float32)
    cols["back"] = np.broadcast_to(np.arange(NT, dtype=np.float32)[None, :] - NT, (P, NT))
    cols["row"] = i.astype(np.float32)
    earlier = (np.arange(E)[None, :] < np.arange(E)[:, None]) * float(P)
    cols["first"] = np.broadcast_to(earlier.reshape(1, E * E).astype(np.float32), (P, E * E))
    params = np.ascontiguousarray(np.concatenate([cols[n] for n in _AT], axis=1))
    experts = np.ascontiguousarray(np.concatenate([
        a["ffn_w1"],
        a["ffn_w2"].reshape(E, FC, P, P).transpose(0, 2, 1, 3).reshape(E, P, FC * P),
        a["ffn_b1"].reshape(E, FC, P).transpose(0, 2, 1),
        np.broadcast_to(a["ffn_b2"][:, None, :], (E, P, P)),
    ], axis=2))
    arrays = {"x": np.ascontiguousarray(a["attn_x"].reshape(B * T, P)), "params": params, "experts": experts}

    nc = bacc.Bacc("TRN2", target_bir_lowering=False, num_devices=1)
    aps = [nc.dram_tensor(n, v.shape, F32, kind="ExternalInput").ap() for n, v in arrays.items()]
    out = nc.dram_tensor("out", (B * T, P), F32, kind="ExternalOutput").ap()
    program(nc, *aps, out)
    r = run(nc, [arrays], core_ids=[0])
    return r.results[0]["out"].reshape(B, T, P)
```
